# Optimizing a Trainium2 kernel written in Bass

```python
import numpy as np
import jax
import jax.numpy as jnp

def _softmax(x, axis=-1):
    return jax.nn.softmax(x, axis=axis)

def _gelu(x):
    return jax.nn.gelu(x, approximate=True)

def _silu(x):
    return jax.nn.silu(x)

def _sigmoid(x):
    return jax.nn.sigmoid(x)

def _layernorm(x, axis=-1, eps=1e-05):
    m = jnp.mean(x, axis=axis, keepdims=True)
    v = jnp.var(x, axis=axis, keepdims=True)
    return (x - m) / jnp.sqrt(v + eps)

def _scatter_add(tgt, idx, src, axis=0):
    return tgt.at[idx].add(src)

def _segment_sum(src, seg, n):
    return jax.ops.segment_sum(src, seg, n)
kernel_name = 'mk_adj_ffn_d1_adj_r2_e0c368'

def setup_inputs(seed: int=0):
    np.random.seed(seed)
    _w = jnp.asarray

    def _rec_inputs():
        import jax
        import jax.numpy as jnp
        _gk = jax.random.key(seed)
        x = -0.0003929 + 0.9999 * jax.random.normal(jax.random.fold_in(_gk, 1), (128, 64, 128), jnp.float32)
        _w = (1.0 + jnp.arange(64, dtype=jnp.float32)) ** (-0.5)
        _w = _w / _w.mean()
        _pij = jnp.clip(0.0625 * _w[:, None] * _w[None, :], 0.0, 1.0)
        _a = jax.random.uniform(jax.random.fold_in(_gk, 2), (64, 64)) < _pij
        _a = jnp.logical_or(_a, jnp.swapaxes(_a, -1, -2))
        _a = jnp.logical_or(_a, jnp.eye(64, dtype=bool))
        _af = _a.astype(jnp.float32)
        _af = _af * jax.random.uniform(jax.random.fold_in(_gk, 3), (64, 64), jnp.float32, 0.05, 1)
        adj = _af
        return (x, adj)
    x, adj = _rec_inputs()

    def _L0_gnn_setup():
        import jax, jax.numpy as jnp
        import numpy as np
        EPS = 1e-05

        def _batchnorm(x, gamma, beta):
            mu = jnp.mean(x, axis=0)
            var = jnp.var(x, axis=0)
            return (x - mu) * jax.lax.rsqrt(var + EPS) * gamma + beta
        key = jax.random.key(seed)
        ks = jax.random.split(key, 4)
        b, n, d, h, o = (32, 1024, 128, 256, 128)
        features = jax.random.normal(ks[0], (b, n, d), dtype=jnp.float32)
        A = jax.random.uniform(ks[1], (n, n), dtype=jnp.float32)
        lim1 = float(np.sqrt(6.0 / (d + h)))
        W1 = jax.random.uniform(ks[2], (h, d), minval=-lim1, maxval=lim1, dtype=jnp.float32)
        b1 = jnp.zeros((h,), jnp.float32)
        lim2 = float(np.sqrt(6.0 / (h + o)))
        W2 = jax.random.uniform(ks[3], (o, h), minval=-lim2, maxval=lim2, dtype=jnp.float32)
        b2 = jnp.zeros((o,), jnp.float32)
        g1 = jnp.ones((h,), jnp.float32)
        be1 = jnp.zeros((h,), jnp.float32)
        g2 = jnp.ones((o,), jnp.float32)
        be2 = jnp.zeros((o,), jnp.float32)
        return {'features': features, 'A': A, 'W1': W1, 'b1': b1, 'g1': g1, 'be1': be1, 'W2': W2, 'b2': b2, 'g2': g2, 'be2': be2}
    _L0_gnn_all = _L0_gnn_setup()
    _L0_gnn_in = {k: v for k, v in _L0_gnn_all.items() if k in ('W1', 'b1', 'g1', 'be1', 'W2', 'b2', 'g2', 'be2')}
    del _L0_gnn_all

    def _L0_ffn_setup():
        import jax, jax.numpy as jnp
        import numpy as np
        N_EXPERTS = 8
        TOP_K = 2
        key = jax.random.key(seed)
        ks = jax.random.split(key, 5)
        B, T, C, E, H = (8, 1024, 128, 8, 341)
        scale = 1.0 / np.sqrt(C)
        return {'x': jax.random.normal(ks[0], (B, T, C), dtype=jnp.float32), 'router_w': jax.random.normal(ks[1], (E, C), dtype=jnp.float32) * scale, 'w1': jax.random.normal(ks[2], (E, H, C), dtype=jnp.float32) * scale, 'w2': jax.random.normal(ks[3], (E, C, H), dtype=jnp.float32) * (1.0 / np.sqrt(H)), 'w3': jax.random.normal(ks[4], (E, H, C), dtype=jnp.float32) * scale}
    _L0_ffn_all = _L0_ffn_setup()
    _L0_ffn_in = {k: v for k, v in _L0_ffn_all.items() if k in ('router_w', 'w1', 'w2', 'w3')}
    del _L0_ffn_all
    return {'x': x, 'adj': adj, 'L0_gnn_W1': _L0_gnn_in['W1'], 'L0_gnn_b1': _L0_gnn_in['b1'], 'L0_gnn_g1': _L0_gnn_in['g1'], 'L0_gnn_be1': _L0_gnn_in['be1'], 'L0_gnn_W2': _L0_gnn_in['W2'], 'L0_gnn_b2': _L0_gnn_in['b2'], 'L0_gnn_g2': _L0_gnn_in['g2'], 'L0_gnn_be2': _L0_gnn_in['be2'], 'L0_ffn_router_w': _L0_ffn_in['router_w'], 'L0_ffn_w1': _L0_ffn_in['w1'], 'L0_ffn_w2': _L0_ffn_in['w2'], 'L0_ffn_w3': _L0_ffn_in['w3']}

def reference(x, adj, L0_gnn_W1, L0_gnn_b1, L0_gnn_g1, L0_gnn_be1, L0_gnn_W2, L0_gnn_b2, L0_gnn_g2, L0_gnn_be2, L0_ffn_router_w, L0_ffn_w1, L0_ffn_w2, L0_ffn_w3):
    import jax
    import jax.numpy as jnp

    def _L0_gnn_ref(features, A, W1, b1, g1, be1, W2, b2, g2, be2):
        import jax, jax.numpy as jnp
        import numpy as np
        EPS = 1e-05

        def _batchnorm(x, gamma, beta):
            mu = jnp.mean(x, axis=0)
            var = jnp.var(x, axis=0)
            return (x - mu) * jax.lax.rsqrt(var + EPS) * gamma + beta
        b, n, d = features.shape
        A_norm = A + jnp.eye(n, dtype=A.dtype)
        deg = jnp.sum(A_norm, axis=0) + jnp.sum(A_norm, axis=1) - jnp.diagonal(A_norm)
        dinv = jax.lax.rsqrt(deg)
        A_hat = A_norm * dinv[:, None] * dinv[None, :]
        agg = jnp.einsum('nm,bmd->bnd', A_hat, features)
        x = agg.reshape(-1, d)
        h = jax.nn.relu(_batchnorm(x @ W1.T + b1, g1, be1))
        out = h @ W2.T + b2
        out = _batchnorm(out, g2, be2)
        return out.reshape(b, n, -1)

    def _L0_ffn_ref(x, router_w, w1, w2, w3):
        import jax, jax.numpy as jnp
        import numpy as np
        N_EXPERTS = 8
        TOP_K = 2
        B, T, C = x.shape
        flat = x.reshape(-1, C)
        logits = flat @ router_w.T
        probs = jax.nn.softmax(logits, axis=-1)
        topk_probs, topk_idx = jax.lax.top_k(probs, TOP_K)
        topk_probs = topk_probs / (jnp.sum(topk_probs, axis=-1, keepdims=True) + 1e-09)
        onehot = jax.nn.one_hot(topk_idx, N_EXPERTS, dtype=flat.dtype)
        gates = jnp.einsum('nk,nke->ne', topk_probs, onehot)
        h1 = jnp.einsum('nc,ehc->neh', flat, w1)
        h3 = jnp.einsum('nc,ehc->neh', flat, w3)
        h = jax.nn.silu(h1) * h3
        y = jnp.einsum('neh,ech->nec', h, w2)
        out = jnp.einsum('ne,nec->nc', gates, y)
        return out.reshape(B, T, C)
    x = x + _L0_gnn_ref(_layernorm(x, axis=-1), adj, L0_gnn_W1, L0_gnn_b1, L0_gnn_g1, L0_gnn_be1, L0_gnn_W2, L0_gnn_b2, L0_gnn_g2, L0_gnn_be2)
    x = x + _L0_ffn_ref(_layernorm(x, axis=-1), L0_ffn_router_w, L0_ffn_w1, L0_ffn_w2, L0_ffn_w3)
    return x

_drawn_inputs = setup_inputs


def setup_inputs(seed=0):
    import zlib

    import numpy as np

    out = dict(_drawn_inputs(seed))
    spreads = {'L0_gnn_b1': (0.0, 0.1),
     'L0_gnn_g1': (1.0, 0.2),
     'L0_gnn_be1': (0.0, 0.1),
     'L0_gnn_b2': (0.0, 0.1),
     'L0_gnn_g2': (1.0, 0.2),
     'L0_gnn_be2': (0.0, 0.1)}
    factors = {}
    for name, (base, spread) in spreads.items():
        noise = np.random.default_rng([zlib.crc32(name.encode()), seed]).standard_normal(out[name].shape)
        drawn = base * np.exp(spread * noise) if base else spread * noise
        out[name] = jnp.asarray(drawn.astype(out[name].dtype))
    for name, factor in factors.items():
        out[name] = (out[name] * factor).astype(out[name].dtype)
    return out
```

```python
import concourse.bass as bass
from concourse import mybir
from contextlib import ExitStack

P = 128
B, N, C = 128, 64, 128
TOK = B * N
T = TOK // P
GT = 4
GR = T // GT
GC = GT * P
QT = T // 4
HID = 256
HALVES = HID // P
E, TOPK, HF = 8, 2, 341
EPS = 1e-5
CHUNKS = (8, 24, 24, 8)
RING = 8
UNIT = 2
UNITS = RING // UNIT
SLOTS = tuple(-(-(TOPK * nt + E - 1) // RING) * RING for nt in CHUNKS)
NS = sum(SLOTS)
ROW = C + 1
HA = 342
HB = 2 * HF - HA
PAD = 512 - HA
KC = 114
KJ = (KC, KC, HF - 2 * KC)


def build(nc, x, adj, gw1, gw2, gvec, rw, w13, w2, out):
    f32, f32r, i32 = mybir.dt.float32, mybir.dt.float32r, mybir.dt.int32
    ACT, ALU, AX = mybir.ActivationFunctionType, mybir.AluOpType, mybir.AxisListType.X
    ds = bass.ds
    V, S = nc.vector, nc.scalar
    chunk0 = [sum(CHUNKS[:c]) for c in range(len(CHUNKS))]
    slot0 = [sum(SLOTS[:c]) for c in range(len(CHUNKS))]
    NTX, NSX = max(CHUNKS), max(SLOTS)

    sent = [nc.dram_tensor(f"sent{c}", [s * P, ROW], f32, kind="Internal").ap() for c, s in enumerate(SLOTS)]
    back = [nc.dram_tensor(f"back{c}", [s * P, C], f32, kind="Internal").ap() for c, s in enumerate(SLOTS)]

    with ExitStack() as ctx:
        def sb(name, shape, dt=f32):
            return ctx.enter_context(nc.sbuf_tensor(name, shape, dt))

        def sem(name):
            return ctx.enter_context(nc.semaphore(name))

        xs = sb("xs", [P, T, C])
        big = sb("big", [P, 2 * TOK + T])
        hid = [big[:, h * TOK:(h + 1) * TOK] for h in range(HALVES)]
        gout = hid[0]
        zrow = big[:, TOK:TOK + T * ROW].rearrange("p (t r) -> p t r", r=ROW)
        w13h, w13l = sb("w13h", [P, E * 2 * HF], f32r), sb("w13l", [P, E * 2 * HF], f32r)
        w2h, w2l = sb("w2h", [KC, E * 3 * C], f32r), sb("w2l", [KC, E * 3 * C], f32r)
        zTh, zTl = sb("zTh", [P, 2, P], f32r), sb("zTl", [P, 2, P], f32r)
        hTh, hTl = sb("hTh", [KC, 2, 3 * P], f32r), sb("hTl", [KC, 2, 3 * P], f32r)

        arena = sb("arena", [P, 2 * QT * C + 2 * GC + 2 * HF + 3 * C])
        at = [0]

        def part(n):
            at[0] += n
            return arena[:, at[0] - n:at[0]]

        fring = part(2 * QT * C).rearrange("p (t c) -> p t c", c=C)
        aggT = part(2 * GC).rearrange("p (b n) -> p b n", b=2)
        st13 = part(2 * HF)
        st2 = part(3 * C)
        at[0] = 0
        zslot = part(RING * ROW).rearrange("p (s r) -> p s r", r=ROW)
        sil = part(2 * HF).rearrange("p (b n) -> p b n", b=2)
        hsl = part(2 * 3 * KC).rearrange("p (b n) -> p b n", b=2)
        ysl = part(RING * C).rearrange("p (s c) -> p s c", c=C)
        zTr = part(2 * GC).rearrange("p (b n) -> p b n", b=2)
        tmp = [part(E * NTX) for _ in range(8)]

        ident, upper, ones = sb("ident", [P, P]), sb("upper", [P, P]), sb("ones", [P, P])
        blk, ahat = sb("blk", [P, P]), sb("ahat", [P, P])
        gw1s, gw2s = sb("gw1s", [P, HID]), sb("gw2s", [P, HALVES, C])
        vec, rws = sb("vec", [P, 9]), sb("rws", [P, E])
        b1, g1, be1 = vec[:, 0:2], vec[:, 2:4], vec[:, 4:6]
        b2, g2, be2 = vec[:, 6:7], vec[:, 7:8], vec[:, 8:9]
        zero = sb("zero", [P, UNIT * ROW])
        st6 = sb("st6", [P, T, 6])
        hst = sb("hst", [P, HALVES, GR * 6])
        ost = sb("ost", [P, GR * 6])
        mean, rstd = sb("mean", [P, T]), sb("rstd", [P, T])
        rv, rs, rt = sb("rv", [P, T]), sb("rs", [P, T]), sb("rt", [P, T])
        mv = sb("mv", [P, HALVES, 2])
        bnsc, bnsh = sb("bnsc", [P, 3]), sb("bnsh", [P, 3])
        deg = sb("deg", [P, 4])
        revi, rev = sb("revi", [P, E], i32), sb("rev", [P, E])
        soi, so = sb("soi", [1, NSX], i32), sb("so", [1, NSX])
        gate2 = sb("gate2", [P, T])
        idx = [sb(f"idx{k}", [P, T], i32) for k in range(TOPK)]
        etab = sb("etab", [1, NS], i32)
        sm = sb("sm", [P, 8, NTX])
        cnt = sb("cnt", [P, 4, E])
        cnti = sb("cnti", [P, 2, E], i32)

        ps = ctx.enter_context(nc.psum_tensor("ps", [P, 8, 512], f32))
        psA = [ps[:, b, :] for b in (0, 1)]
        psH = [ps[:, 2 + 2 * b:4 + 2 * b, :] for b in (0, 1)]
        psT = [ps[:, b, :] for b in (2, 3)]
        psZ = [ps[:, b, :] for b in (4, 5)]
        psL = [ps[:, b, :] for b in (6, 7)]
        psR = ps[:, 0, :]
        flat = ps[:, :, :].rearrange("p b n -> p (b n)")
        ps13 = [flat[:, 1024 * b + PAD:1024 * b + PAD + 2 * HF] for b in (0, 1)]
        psz = ps[:, 4, 0:P]
        psh = [ps[0:KC, 5 + b, 0:3 * P] for b in (0, 1)]
        psy = ps[:, 7, 0:C]

        x_in = [sem(f"x_in{q}") for q in range(4)]
        adj_in, par_in = sem("adj_in"), sem("par_in")
        stage13_in, stage2_in = sem("stage13_in"), sem("stage2_in")
        zeroed = sem("zeroed")
        consts, cleared = sem("consts"), sem("cleared")
        split = sem("split")
        stat_ok = sem("stat_ok")
        dseq = sem("dseq")
        root_in, root_out = sem("root_in"), sem("root_out")
        adj_col, adj_sc, adj_T, adj_ok = sem("adj_col"), sem("adj_sc"), sem("adj_T"), sem("adj_ok")
        f_ready, agg_mm, agg_ev = sem("f_ready"), sem("agg_mm"), sem("agg_ev")
        hid_mm, hid_ev = sem("hid_mm"), sem("hid_ev")
        bn1_ok, bn2_ok, relu_ok = sem("bn1_ok"), sem("bn2_ok"), sem("relu_ok")
        out_mm, out_ev, ostat = sem("out_mm"), sem("out_ev"), sem("ostat")
        bnout, outT_mm, x2_ok = sem("bnout"), sem("outT_mm"), sem("x2_ok")
        z_ok, zr_mm, zr_ev, logit_mm = sem("z_ok"), sem("zr_mm"), sem("zr_ev"), sem("logit_mm")
        ex_in, ex_out = sem("ex_in"), sem("ex_out")
        sel_ok, rank_mm, routed = sem("sel_ok"), sem("rank_mm"), sem("routed")
        sent_k = [sem(f"sent_k{k}") for k in range(TOPK)]
        regate = sem("regate")
        slot_in = [sem(f"slot_in{u}") for u in range(UNITS)]
        slot_out = [sem(f"slot_out{u}") for u in range(UNITS)]
        zT_mm, zh_ok, zl_ok = sem("zT_mm"), sem("zh_ok"), sem("zl_ok")
        h13_mm, silu_ok, h_ok = sem("h13_mm"), sem("silu_ok"), sem("h_ok")
        hT_mm, hTh_ok, hTl_ok = sem("hT_mm"), sem("hTh_ok"), sem("hTl_ok")
        y_mm, y_ev = sem("y_mm"), sem("y_ev")
        got_k = [sem(f"got_k{k}") for k in range(TOPK)]
        stored = sem("stored")

        block = ctx.enter_context(nc.Block())

        @block.sync
        def _(sp):
            xv = x.rearrange("(t p) c -> p t c", p=P)
            sp.dma_start(xs[:, 0:QT, :], xv[:, 0:QT, :]).then_inc(x_in[0], 16)
            sp.wait_ge(cleared, 1)
            sp.dma_start(blk[0:N, 0:N], adj).then_inc(adj_in, 16)
            sp.dma_start(blk[N:P, N:P], adj).then_inc(adj_in, 16)
            sp.dma_start(gw1s[:, :], gw1).then_inc(par_in, 16)
            sp.dma_start(gw2s[:, :, :], gw2.rearrange("(h p) o -> p h o", p=P)).then_inc(par_in, 16)
            sp.dma_start(vec[:, :], gvec).then_inc(par_in, 16)
            sp.dma_start(rws[:, :], rw).then_inc(par_in, 16)
            for q in range(1, 4):
                sp.dma_start(xs[:, q * QT:(q + 1) * QT, :], xv[:, q * QT:(q + 1) * QT, :]).then_inc(x_in[q], 16)
            with sp.Fori(0, E) as e:
                sp.wait_ge(split, e * 4 + 1)
                sp.dma_start(st13, w13[:, ds(e * (2 * HF), 2 * HF)]).then_inc(stage13_in, 16)
                sp.dma_start(st2[0:KC, :].rearrange("p (j c) -> p j c", j=3)[:, 0:2, :],
                             w2[ds(e * HF, 2 * KC), :].rearrange("(j p) c -> p j c", p=KC)).then_inc(stage2_in, 16)
                sp.dma_start(st2[0:KJ[2], 2 * C:3 * C], w2[ds(e * HF + 2 * KC, KJ[2]), :]).then_inc(stage2_in, 16)

            def step(src, u, src_row, dst, dst_row, done):
                if done is not None:
                    sp.wait_ge(y_ev, done)
                if dst is not None:
                    sp.dma_start(dst[ds(dst_row, UNIT * P), :].rearrange("(s p) c -> p s c", p=P),
                                 ysl[:, UNIT * u:UNIT * u + UNIT, :]).then_inc(slot_out[u], 16)
                if src is not None:
                    sp.dma_start(zslot[:, UNIT * u:UNIT * u + UNIT, :],
                                 src[ds(src_row, UNIT * P), :].rearrange("(s p) c -> p s c", p=P)).then_inc(slot_in[u], 16)

            for c in range(len(CHUNKS)):
                for k in range(TOPK):
                    sp.wait_ge(sent_k[k], 16 * (chunk0[c] + CHUNKS[c]))
                for u in range(UNITS):
                    n = slot0[c] // UNIT + u
                    step(sent[c], u, u * UNIT * P,
                         back[c - 1] if c else None, (SLOTS[c - 1] - RING + u * UNIT) * P if c else None,
                         UNIT * (n - UNITS + 1) if c else None)
                with sp.Fori(1, SLOTS[c] // RING) as r:
                    for u in range(UNITS):
                        step(sent[c], u, r * (RING * P) + u * UNIT * P,
                             back[c], r * (RING * P) + (u * UNIT - RING) * P,
                             r * RING + (slot0[c] + u * UNIT - RING + UNIT))
            for u in range(UNITS):
                step(None, u, None, back[-1], (SLOTS[-1] - RING + u * UNIT) * P, NS - RING + (u + 1) * UNIT)

        @block.gpsimd
        def _(gp):
            gp.memset(blk[:, :], 0.0).then_inc(cleared, 1)
            gp.memset(st2, 0.0).then_inc(split, 1)
            gp.memset(zero[:, :], 0.0).then_inc(consts, 1)
            gp.memset(ident[:, :], 0.0).then_inc(consts, 1)
            gp.memset(ones[:, :], 1.0).then_inc(consts, 1)
            gp.iota(revi[:, :], [[-1, E]], base=E, channel_multiplier=0).then_inc(consts, 1)
            gp.iota(soi[:, :], [[1, NSX]], base=0, channel_multiplier=0).then_inc(consts, 1)
            gp.wait_ge(consts, 5)
            gp.affine_select(out=ident[:, :], in_=ident[:, :], compare_op=ALU.not_equal, fill=1.0,
                             base=0, pattern=[[-1, P]], channel_multiplier=1).then_inc(consts, 1)
            gp.affine_select(out=upper[:, :], in_=ones[:, :], compare_op=ALU.is_gt, fill=0.0,
                             base=0, pattern=[[1, P]], channel_multiplier=-1).then_inc(consts, 1)
            gp.tensor_copy(rev[:, :], revi[:, :]).then_inc(consts, 1)
            gp.tensor_copy(so[:, :], soi[:, :]).then_inc(consts, 1)
            for c, s in enumerate(SLOTS):
                gp.dma_start(sent[c].rearrange("(p a s) r -> p a (s r)", p=P, s=UNIT),
                             zero[:, :].unsqueeze(1).broadcast_to([P, s // UNIT, UNIT * ROW])).then_inc(zeroed, 16)
            with gp.Fori(0, E) as e:
                gp.wait_ge(stage13_in, e * 16 + 16)
                a = ds(e * (2 * HF), 2 * HF)
                gp.tensor_copy(w13h[:, a], st13).then_inc(split, 1)
                gp.wait_ge(split, e * 4 + 2)
                gp.tensor_tensor(w13l[:, a], st13, w13h[:, a].bitcast(f32), ALU.subtract).then_inc(split, 1)
                gp.wait_ge(stage2_in, e * 32 + 32)
                b = ds(e * (3 * C), 3 * C)
                gp.tensor_copy(w2h[:, b], st2[0:KC, :]).then_inc(split, 1)
                gp.wait_ge(split, e * 4 + 4)
                gp.tensor_tensor(w2l[:, b], st2[0:KC, :], w2h[:, b].bitcast(f32), ALU.subtract).then_inc(split, 1)
            gp.wait_ge(zeroed, 16 * len(CHUNKS))
            for c, nt in enumerate(CHUNKS):
                gp.wait_ge(routed, c + 1)
                tiles = slice(chunk0[c], chunk0[c] + nt)
                for k in range(TOPK):
                    if k:
                        gp.wait_ge(sent_k[0], 16 * (chunk0[c] + nt))
                        gp.tensor_copy(zrow[:, tiles, C], gate2[:, tiles]).then_inc(regate, 1)
                        gp.wait_ge(regate, c + 1)
                    for t in range(chunk0[c], chunk0[c] + nt):
                        gp.indirect_dma_start(sent[c], bass.IndirectOffsetOnAxis(idx[k][:, t:t + 1], 0),
                                              zrow[:, t, :], None).then_inc(sent_k[k], 16)
            ov = out.rearrange("(t p) c -> p t c", p=P)
            for c, nt in enumerate(CHUNKS):
                tiles = slice(chunk0[c], chunk0[c] + nt)
                for u in range(UNITS):
                    gp.wait_ge(slot_out[u], 16 * ((slot0[c] + SLOTS[c]) // RING))
                for k in range(TOPK):
                    for t in range(chunk0[c], chunk0[c] + nt):
                        gp.indirect_dma_start(xs[:, t, :], None, back[c],
                                              bass.IndirectOffsetOnAxis(idx[k][:, t:t + 1], 0),
                                              compute_op=ALU.add).then_inc(got_k[k], 16)
                    gp.wait_ge(got_k[k], 16 * (chunk0[c] + nt))
                gp.dma_start(ov[:, tiles, :], xs[:, tiles, :]).then_inc(stored, 16)
            gp.wait_ge(stored, 16 * len(CHUNKS))

        @block.scalar
        def _(act):
            roots = [0]

            def root(cols):
                roots[0] += 1
                act.wait_ge(root_in, roots[0])
                S.activation(rs[:, cols], rv[:, cols], ACT.Sqrt).then_inc(root_out, 1)

            root(slice(0, 1))
            root(slice(0, QT))
            root(slice(QT, 2 * QT))

            def agg_out(g, b, first=False):
                act.wait_ge(agg_mm, g + 1)
                if not first:
                    act.wait_ge(hid_mm, g * 2 - 2)
                S.activation(aggT[:, b, :], psA[b], ACT.Copy).then_inc(agg_ev, 1)

            def hid_out(g, b):
                for h in range(HALVES):
                    act.wait_ge(hid_mm, g * 2 + (h + 1))
                    S.activation(hid[h][:, ds(g * GC, GC)], psH[b][:, h, :], ACT.Identity,
                                 bias=b1[:, h:h + 1]).then_inc(hid_ev, 1)

            act.wait_ge(par_in, 64)
            agg_out(0, 0, True)
            for q in range(4):
                lo, hi = q * QT // GT, (q + 1) * QT // GT
                if q == 0:
                    agg_out(1, 1, True)
                    hid_out(0, 0)
                    agg_out(2, 0)
                    hid_out(1, 1)
                    lo += 2
                last = q == 3
                with act.Fori(lo // 2, hi // 2 - last) as j:
                    agg_out(j * 2 + 1, 1)
                    hid_out(j * 2, 0)
                    agg_out(j * 2 + 2, 0)
                    hid_out(j * 2 + 1, 1)
                if last:
                    agg_out(GR - 1, 1)
                    hid_out(GR - 2, 0)
                    hid_out(GR - 1, 1)
                if q < 2:
                    root(slice((q + 2) * QT, (q + 3) * QT))
            root(slice(0, 2))
            act.wait_ge(bn1_ok, 1)
            with act.Fori(0, GR) as g:
                for h in range(HALVES):
                    S.activation(hid[h][:, ds(g * GC, GC)], hid[h][:, ds(g * GC, GC)], ACT.Relu,
                                 bias=bnsh[:, h:h + 1], scale=bnsc[:, h:h + 1]).then_inc(relu_ok, 1)
            root(slice(0, 1))
            act.wait_ge(bn2_ok, 1)

            def bn_apply(g0, g1):
                with act.Fori(g0, g1) as g:
                    a = gout[:, ds(g * GC, GC)]
                    S.activation(a, a, ACT.Identity, bias=bnsh[:, 2:3], scale=bnsc[:, 2:3]).then_inc(bnout, 1)

            def zr_out(g, b, first):
                act.wait_ge(zr_mm, g + 1)
                if not first:
                    act.wait_ge(logit_mm, g - 1)
                S.activation(zTr[:, b, :], psZ[b], ACT.Copy).then_inc(zr_ev, 1)

            bn_apply(0, CHUNKS[0] // GT)
            for c, nt in enumerate(CHUNKS):
                g0, ng = chunk0[c] // GT, nt // GT
                root(slice(chunk0[c], chunk0[c] + nt))
                if c + 1 < len(CHUNKS):
                    bn_apply(g0 + ng, g0 + ng + CHUNKS[c + 1] // GT)
                if c == 0:
                    zr_out(0, 0, True)
                    zr_out(1, 1, True)
                    g0, ng = g0 + 2, ng - 2
                if ng:
                    with act.Fori(g0 // 2, (g0 + ng) // 2) as j:
                        zr_out(j * 2, 0, False)
                        zr_out(j * 2 + 1, 1, False)
                act.wait_ge(ex_in, c + 1)
                S.activation(tmp[0][:, 0:E * nt], tmp[0][:, 0:E * nt], ACT.Exp).then_inc(ex_out, 1)

            def z_hi(g, i, first=False):
                act.wait_ge(zT_mm, g + 1)
                if not first:
                    act.wait_ge(h13_mm, g - 1)
                S.activation(zTh[:, i % 2, :], psz, ACT.Copy).then_inc(zh_ok, 1)

            def silu(g, i, first=False):
                act.wait_ge(h13_mm, g + 1)
                if not first:
                    act.wait_ge(h_ok, g - 1)
                S.activation(sil[:, i % 2, :], ps13[i % 2][:, 0:HF], ACT.Silu).then_inc(silu_ok, 1)

            def hT_hi(g, i, first=False):
                act.wait_ge(hT_mm, g + 1)
                if not first:
                    act.wait_ge(y_mm, g - 1)
                S.activation(hTh[:, i % 2, :], psh[i % 2], ACT.Copy).then_inc(hTh_ok, 1)

            def y_out(g, i, used):
                act.wait_ge(y_mm, g + 1)
                if used is not None and i % UNIT == 0:
                    act.wait_ge(slot_out[i // UNIT], used)
                S.activation(ysl[:, i, :], psy, ACT.Copy, scale=zslot[:, i, C:ROW]).then_inc(y_ev, 1)

            z_hi(0, 0, True)
            for g in range(2 * RING):
                z_hi(g + 1, g + 1, g == 0)
                silu(g, g, g < 2)
                if g >= 1:
                    hT_hi(g - 1, g - 1, g < 3)
                if g >= 2:
                    y_out(g - 2, (g - 2) % RING, 16 if g - 2 >= RING else None)
            with act.Fori(2, NS // RING - 1) as r:
                for i in range(RING):
                    g = r * RING + i
                    z_hi(g + 1, i + 1)
                    silu(g, i)
                    hT_hi(g - 1, i - 1)
                    y_out(g - 2, (i - 2) % RING, r * 16 if i >= 2 else r * 16 - 16)
            for i in range(RING + 2):
                g = NS - RING + i
                if i < RING - 1:
                    z_hi(g + 1, i + 1)
                if i < RING:
                    silu(g, i)
                if i < RING + 1:
                    hT_hi(g - 1, i - 1)
                y_out(g - 2, (i - 2) % RING, 16 * ((g - 2) // RING))

        @block.vector
        def _(dve):
            seq, roots, seen = [0], [0], [0]

            def link(ins):
                seq[0] += 1
                ins.then_inc(dseq, 1)
                dve.wait_ge(dseq, seq[0])

            def stats(groups):
                seen[0] += groups
                dve.wait_ge(stat_ok, seen[0])

            def rsqrt(dst, cols):
                roots[0] += 1
                a = rv[:, cols]
                dve.wait_ge(root_out, roots[0])
                link(V.reciprocal(dst, rs[:, cols]))
                link(V.tensor_tensor(rt[:, cols], dst, dst, ALU.mult))
                link(V.tensor_tensor(rt[:, cols], rt[:, cols], a, ALU.mult))
                link(V.tensor_scalar(rt[:, cols], rt[:, cols], -0.5, 1.5, ALU.mult, ALU.add))
                link(V.tensor_tensor(dst, dst, rt[:, cols], ALU.mult))

            dve.wait_ge(consts, 9)
            dve.wait_ge(adj_in, 32)
            link(V.tensor_tensor(blk[:, :], blk[:, :], ident[:, :], ALU.add))
            V.tensor_reduce(deg[:, 0:1], blk[:, :], AX, ALU.add).then_inc(adj_sc, 1)
            link(V.tensor_tensor(ahat[:, :], blk[:, :], ident[:, :], ALU.mult))
            link(V.tensor_reduce(deg[:, 1:2], ahat[:, :], AX, ALU.add))
            link(V.tensor_tensor(deg[:, 2:3], deg[:, 0:1], deg[:, 1:2], ALU.subtract))
            dve.wait_ge(adj_col, 1)
            V.tensor_tensor(rv[:, 0:1], psA[0][:, 0:1], deg[:, 2:3], ALU.add).then_inc(root_in, 1)
            rsqrt(deg[:, 3:4], slice(0, 1))
            V.tensor_scalar(blk[:, :], blk[:, :], deg[:, 3:4], None, ALU.mult).then_inc(adj_sc, 1)
            dve.wait_ge(adj_T, 1)
            V.tensor_scalar(ahat[:, :], psA[1][:, 0:P], deg[:, 3:4], None, ALU.mult).then_inc(adj_ok, 1)

            def ln_stats(t0, n):
                cols = slice(t0, t0 + n)
                s = st6[:, cols, :]
                link(V.tensor_tensor(rs[:, cols], s[:, :, 1], s[:, :, 4], ALU.subtract))
                link(V.tensor_tensor(rt[:, cols], rs[:, cols], rs[:, cols], ALU.mult))
                link(V.tensor_tensor(mean[:, cols], s[:, :, 1], s[:, :, 4], ALU.add))
                link(V.tensor_scalar(mean[:, cols], mean[:, cols], 0.5, None, ALU.mult))
                link(V.tensor_tensor(rv[:, cols], s[:, :, 2], s[:, :, 5], ALU.add))
                link(V.tensor_scalar(rv[:, cols], rv[:, cols], 1.0 / C, EPS, ALU.mult, ALU.add))
                V.scalar_tensor_tensor(rv[:, cols], rt[:, cols], 0.25, rv[:, cols], ALU.mult, ALU.add).then_inc(root_in, 1)

            def ln_in(q):
                dve.wait_ge(x_in[q], 16)
                with dve.Fori(q * QT // GT, (q + 1) * QT // GT) as g:
                    for u in range(GT):
                        ins = V.bn_stats(st6[:, g * GT + u, :], xs[:, g * GT + u, :])
                    ins.then_inc(stat_ok, 1)
                stats(QT // GT)
                ln_stats(q * QT, QT)
                cols = slice(q * QT, (q + 1) * QT)
                rsqrt(rstd[:, cols], cols)
                if q >= 2:
                    dve.wait_ge(agg_mm, (q - 1) * QT // GT)
                with dve.Fori(0, QT // GT) as g:
                    for u in range(GT):
                        t = g * GT + (q * QT + u)
                        ins = V.tensor_scalar(fring[:, g * GT + ((q % 2) * QT + u), :], xs[:, t, :],
                                              mean[:, ds(t, 1)], rstd[:, ds(t, 1)], ALU.subtract, ALU.mult)
                    ins.then_inc(f_ready, 1)

            def hid_stats(q):
                with dve.Fori(q * QT // GT, (q + 1) * QT // GT) as g:
                    for h in range(HALVES):
                        dve.wait_ge(hid_ev, g * 2 + (h + 1))
                        ins = V.bn_stats(hst[:, h, ds(g * 6, 6)], hid[h][:, ds(g * GC, GC)])
                    ins.then_inc(stat_ok, 1)
                stats(QT // GT)

            ln_in(0)
            ln_in(1)
            hid_stats(0)
            ln_in(2)
            hid_stats(1)
            ln_in(3)
            hid_stats(2)
            hid_stats(3)

            def bn_finish(n, gamma, beta, at, done):
                V.tensor_scalar(rv[:, 0:n], mv[:, 0:n, 1], EPS, None, ALU.add).then_inc(root_in, 1)
                rsqrt(rstd[:, 0:n], slice(0, n))
                link(V.tensor_tensor(bnsc[:, at:at + n], rstd[:, 0:n], gamma, ALU.mult))
                link(V.tensor_tensor(rt[:, 0:n], mv[:, 0:n, 0], bnsc[:, at:at + n], ALU.mult))
                V.tensor_tensor(bnsh[:, at:at + n], beta, rt[:, 0:n], ALU.subtract).then_inc(done, 1)

            for h in range(HALVES):
                link(V.bn_aggr(mv[:, h, :], hst[:, h, :]))
            bn_finish(2, g1, be1, 0, bn1_ok)

            def gout_out(g, b):
                dve.wait_ge(out_mm, g + 1)
                a = gout[:, ds(g * GC, GC)]
                V.tensor_scalar(a, psA[b], b2, None, ALU.add).then_inc(out_ev, 1)
                dve.wait_ge(out_ev, g + 1)
                V.bn_stats(ost[:, ds(g * 6, 6)], a).then_inc(stat_ok, 1)

            with dve.Fori(0, GR // 2) as j:
                gout_out(j * 2, 0)
                gout_out(j * 2 + 1, 1)
            stats(GR)
            link(V.bn_aggr(mv[:, 0, :], ost[:, :]))
            bn_finish(1, g2, be2, 2, bn2_ok)

            def residual(g, b):
                dve.wait_ge(outT_mm, g + 1)
                a = xs[:, ds(g * GT, GT), :].rearrange("p t c -> p (t c)")
                V.tensor_tensor(a, psT[b], a, ALU.add).then_inc(x2_ok, 1)
                dve.wait_ge(x2_ok, g + 1)
                for u in range(GT):
                    ins = V.bn_stats(st6[:, g * GT + u, :], xs[:, g * GT + u, :])
                ins.then_inc(stat_ok, 1)

            def residuals(c):
                g0 = chunk0[c] // GT
                with dve.Fori(g0 // 2, (g0 + CHUNKS[c] // GT) // 2) as j:
                    residual(j * 2, 0)
                    residual(j * 2 + 1, 1)
                stats(CHUNKS[c] // GT)

            def normalise(c):
                t0, nt = chunk0[c], CHUNKS[c]
                ln_stats(t0, nt)
                rsqrt(rstd[:, t0:t0 + nt], slice(t0, t0 + nt))
                with dve.Fori(t0 // GT, (t0 + nt) // GT) as g:
                    for u in range(GT):
                        t = g * GT + u
                        ins = V.tensor_scalar(zrow[:, t, 0:C], xs[:, t, :], mean[:, ds(t, 1)], rstd[:, ds(t, 1)],
                                              ALU.subtract, ALU.mult)
                    ins.then_inc(z_ok, 1)

            def route(c):
                t0, nt, ns = chunk0[c], CHUNKS[c], SLOTS[c]
                n = E * nt
                et = lambda a: a[:, 0:n].rearrange("p (e t) -> p e t", t=nt)
                te = lambda a: a[:, 0:n].rearrange("p (e t) -> p t e", t=nt)
                over_e = lambda a: a.unsqueeze(1).broadcast_to([P, E, nt])
                over_t = lambda a: a.unsqueeze(2).broadcast_to([P, E, nt])
                mx, s, v1, k1, v2, den = (sm[:, i, 0:nt] for i in range(6))
                pr, key, m1, pm, m2, both, inc, pf = tmp
                dve.wait_ge(logit_mm, (t0 + nt) // GT)
                lg = psL[c % 2][:, 0:n].rearrange("p (t e) -> p t e", e=E)
                link(V.tensor_reduce(mx, lg, AX, ALU.max))
                V.tensor_tensor(et(pr), lg.rearrange("p t e -> p e t"), over_e(mx), ALU.subtract).then_inc(ex_in, 1)
                dve.wait_ge(ex_out, c + 1)
                link(V.tensor_reduce(s, te(pr), AX, ALU.add))
                link(V.tensor_reduce(v1, te(pr), AX, ALU.max))
                link(V.tensor_tensor(et(key), et(pr), over_e(v1), ALU.is_equal))
                link(V.tensor_tensor(et(key), et(key), over_t(rev[:, :]), ALU.mult))
                link(V.tensor_reduce(k1, te(key), AX, ALU.max))
                link(V.tensor_tensor(et(m1), over_t(rev[:, :]), over_e(k1), ALU.is_equal))
                link(V.scalar_tensor_tensor(pm[:, 0:n], m1[:, 0:n], -2.0, pr[:, 0:n], ALU.mult, ALU.add))
                link(V.tensor_reduce(v2, te(pm), AX, ALU.max))
                link(V.tensor_tensor(et(key), et(pm), over_e(v2), ALU.is_equal))
                link(V.tensor_tensor(et(key), et(key), over_t(rev[:, :]), ALU.mult))
                link(V.tensor_reduce(k1, te(key), AX, ALU.max))
                link(V.tensor_tensor(et(m2), over_t(rev[:, :]), over_e(k1), ALU.is_equal))
                V.tensor_tensor(both[:, 0:n], m1[:, 0:n], m2[:, 0:n], ALU.add).then_inc(sel_ok, 1)
                link(V.tensor_tensor(den, v1, v2, ALU.add))
                link(V.scalar_tensor_tensor(den, s, 1e-9, den, ALU.mult, ALU.add))
                link(V.reciprocal(den, den))
                link(V.tensor_tensor(zrow[:, t0:t0 + nt, C], v1, den, ALU.mult))
                link(V.tensor_tensor(gate2[:, t0:t0 + nt], v2, den, ALU.mult))
                rank, tot = psR[:, 0:n], psR[:, n:2 * n]
                cn, nb, cum, off = (cnt[:, i, :] for i in range(4))
                dve.wait_ge(rank_mm, c + 1)
                link(V.tensor_tensor_scan(inc[:, 0:n], ones[:, 0:1].broadcast_to([P, n]), tot, 0.0, ALU.mult, ALU.add))
                link(V.tensor_reduce(cn, tot.rearrange("p (e t) -> p e t", t=nt), AX, ALU.add))
                link(V.tensor_scalar(cnti[:, 0, :], cn, float(P - 1), None, ALU.add))
                link(V.tensor_scalar(cnti[:, 1, :], cnti[:, 0, :], P.bit_length() - 1, None, ALU.arith_shift_right))
                link(V.tensor_copy(nb, cnti[:, 1, :]))
                link(V.tensor_tensor_scan(cum, ones[:, 0:E], nb, 0.0, ALU.mult, ALU.add))
                link(V.tensor_tensor(inc[:, 0:n], inc[:, 0:n], tot, ALU.subtract))
                link(V.tensor_tensor(off, cum, nb, ALU.subtract))
                link(V.scalar_tensor_tensor(off, off, float(P), et(inc)[:, :, 0], ALU.mult, ALU.subtract))
                link(V.tensor_tensor(pf[:, 0:n], rank, inc[:, 0:n], ALU.add))
                link(V.tensor_tensor(et(pf), et(pf), over_t(off), ALU.add))
                for k, m in enumerate((m1, m2)):
                    link(V.tensor_tensor(key[:, 0:n], m[:, 0:n], pf[:, 0:n], ALU.mult))
                    link(V.tensor_reduce(k1, te(key), AX, ALU.add))
                    link(V.tensor_copy(idx[k][:, t0:t0 + nt], k1))
                es = tmp[3][0:1, 0:ns]
                cmp = arena[0:1, 3424 + 1024:3424 + 1024 + E * ns].rearrange("p (s e) -> p s e", e=E)
                link(V.tensor_tensor(cmp, so[0:1, 0:ns].unsqueeze(2).broadcast_to([1, ns, E]),
                                     cum[0:1, :].unsqueeze(1).broadcast_to([1, ns, E]), ALU.is_ge))
                link(V.tensor_reduce(es, cmp, AX, ALU.add))
                V.tensor_scalar(etab[0:1, slot0[c]:slot0[c] + ns], es, float(E - 1), None, ALU.min).then_inc(routed, 1)

            dve.wait_ge(split, 4 * E + 1)
            residuals(0)
            normalise(0)
            for c in range(len(CHUNKS)):
                if c + 1 < len(CHUNKS):
                    residuals(c + 1)
                route(c)
                dve.wait_ge(routed, c + 1)
                if c + 1 < len(CHUNKS):
                    normalise(c + 1)
            link(V.memset(hsl[:, :, HF:3 * KC], 0.0))

            def z_lo(g, i):
                dve.wait_ge(zh_ok, g + 1)
                V.tensor_tensor(zTl[:, i % 2, :], psz, zTh[:, i % 2, :].bitcast(f32), ALU.subtract).then_inc(zl_ok, 1)

            def gated(g, i, first=False):
                dve.wait_ge(silu_ok, g + 1)
                if not first:
                    dve.wait_ge(hT_mm, g - 1)
                V.tensor_tensor(hsl[:, i % 2, 0:HF], ps13[i % 2][:, HF:2 * HF], sil[:, i % 2, :], ALU.mult).then_inc(h_ok, 1)

            def hT_lo(g, i):
                dve.wait_ge(hTh_ok, g + 1)
                V.tensor_tensor(hTl[:, i % 2, :], psh[i % 2], hTh[:, i % 2, :].bitcast(f32), ALU.subtract).then_inc(hTl_ok, 1)

            z_lo(0, 0)
            for g in range(2):
                z_lo(g + 1, g + 1)
                gated(g, g, True)
                if g:
                    hT_lo(g - 1, g - 1)
            with dve.Fori(1, NS // 2 - 1) as r:
                for i in range(2):
                    z_lo(r * 2 + (i + 1), i + 1)
                    gated(r * 2 + i, i)
                    hT_lo(r * 2 + (i - 1), i + 1)
            z_lo(NS - 1, 1)
            gated(NS - 2, 0)
            hT_lo(NS - 3, 1)
            gated(NS - 1, 1)
            hT_lo(NS - 2, 0)
            hT_lo(NS - 1, 1)

        @block.tensor
        def _(pe):
            mm = nc.tensor.matmul
            dve_sc = [0]
            pe.wait_ge(adj_sc, 1)
            mm(psA[0][:, 0:1], blk[:, :], ones[:, 0:1], start=True, stop=True).then_inc(adj_col, 1)
            pe.wait_ge(adj_sc, 2)
            nc.tensor.transpose(psA[1][:, 0:P], blk[:, :], ident[:, :]).then_inc(adj_T, 1)
            pe.wait_ge(adj_ok, 1)
            pe.wait_ge(par_in, 64)

            def agg(g, b, ring, first=False):
                pe.wait_ge(f_ready, g + 1)
                if not first:
                    pe.wait_ge(agg_ev, g - 1)
                for u in range(GT):
                    ins = mm(psA[b][:, u * P:(u + 1) * P], fring[:, ring + u, :], ahat[:, :], start=True, stop=True)
                ins.then_inc(agg_mm, 1)

            def hidden(g, b, first=False):
                pe.wait_ge(agg_ev, g + 1)
                if not first:
                    pe.wait_ge(hid_ev, g * 2 - 2)
                for h in range(HALVES):
                    mm(psH[b][:, h, :], gw1s[:, h * P:(h + 1) * P], aggT[:, b, :], start=True, stop=True).then_inc(hid_mm, 1)

            R8 = 2 * QT // GT
            agg(0, 0, 0, True)
            for half in range(2):
                for j in range(R8 // 2):
                    g = half * R8 + 2 * j
                    agg(g + 1, 1, (2 * j + 1) * GT, g == 0)
                    hidden(g, 0, g == 0)
                    if g + 2 < GR:
                        agg(g + 2, 0, (2 * j + 2) * GT % (2 * QT))
                    hidden(g + 1, 1, g == 0)

            def graph_out(g, b):
                pe.wait_ge(out_ev, g - 1)
                for h in range(HALVES):
                    pe.wait_ge(relu_ok, g * 2 + (h + 1))
                    ins = mm(psA[b], gw2s[:, h, :], hid[h][:, ds(g * GC, GC)], start=(h == 0), stop=(h == HALVES - 1))
                ins.then_inc(out_mm, 1)

            for g in range(2):
                pe.wait_ge(relu_ok, 2 * g + 2)
                for h in range(HALVES):
                    ins = mm(psA[g], gw2s[:, h, :], hid[h][:, g * GC:(g + 1) * GC], start=(h == 0), stop=(h == HALVES - 1))
                ins.then_inc(out_mm, 1)
            with pe.Fori(1, GR // 2) as j:
                graph_out(j * 2, 0)
                graph_out(j * 2 + 1, 1)

            def back_to_rows(g, b, first=False):
                pe.wait_ge(bnout, g + 1)
                if not first:
                    pe.wait_ge(x2_ok, g - 1)
                for u in range(GT):
                    ins = nc.tensor.transpose(psT[b][:, u * P:(u + 1) * P], gout[:, ds(g * GC + u * P, P)], ident[:, :])
                ins.then_inc(outT_mm, 1)

            def z_cols(g, b, first=False):
                pe.wait_ge(z_ok, g + 1)
                if not first:
                    pe.wait_ge(zr_ev, g - 1)
                for u in range(GT):
                    ins = nc.tensor.transpose(psZ[b][:, u * P:(u + 1) * P], zrow[:, g * GT + u, 0:C], ident[:, :])
                ins.then_inc(zr_mm, 1)

            def logits(g, b, c):
                pe.wait_ge(zr_ev, g + 1)
                for u in range(GT):
                    ins = mm(psL[c % 2][:, ds((g * GT + (u - chunk0[c])) * E, E)], zTr[:, b, u * P:(u + 1) * P],
                             rws[:, :], start=True, stop=True)
                ins.then_inc(logit_mm, 1)

            def rows(c):
                g0 = chunk0[c] // GT
                ng = CHUNKS[c] // GT
                for g in range(g0, g0 + ng):
                    back_to_rows(g, g % 2, g < 2)

            def ranks(c):
                n = E * CHUNKS[c]
                pe.wait_ge(sel_ok, c + 1)
                if c:
                    pe.wait_ge(routed, c)
                mm(psR[:, 0:n], upper[:, :], tmp[5][:, 0:n], start=True, stop=True)
                mm(psR[:, n:2 * n], ones[:, :], tmp[5][:, 0:n], start=True, stop=True).then_inc(rank_mm, 1)

            rows(0)
            for c in range(len(CHUNKS)):
                g0, ng = chunk0[c] // GT, CHUNKS[c] // GT
                if c >= 1:
                    ranks(c - 1)
                if c >= 2:
                    pe.wait_ge(routed, c - 1)
                for g in range(g0, g0 + ng, 2):
                    z_cols(g, 0, g < 2)
                    z_cols(g + 1, 1, g < 2)
                    logits(g, 0, c)
                    logits(g + 1, 1, c)
                if c + 1 < len(CHUNKS):
                    rows(c + 1)
            ranks(len(CHUNKS) - 1)
            pe.wait_ge(routed, len(CHUNKS))
            pe.wait_ge(split, 4 * E + 1)

            def zT(g, i, turn, first=False):
                if not first:
                    pe.wait_ge(zl_ok, g)
                if i % UNIT == 0:
                    pe.wait_ge(slot_in[i // UNIT], turn)
                nc.tensor.transpose(psz, zslot[:, i, 0:C], ident[:, :]).then_inc(zT_mm, 1)

            def h13(g, i, e, first=False):
                pe.wait_ge(zl_ok, g + 1)
                if not first:
                    pe.wait_ge(h_ok, g - 1)
                b = i % 2
                zh, zl = zTh[:, b, :], zTl[:, b, :]
                col = e * (2 * HF)
                parts = ((ps13[b][:, 0:HA], 0, HA), (ps13[b][:, HA:2 * HF], HA, HB))
                for z, w, st, sp_ in ((zh, w13h, True, False), (zh, w13l, False, False), (zl, w13h, False, True)):
                    for o, c0, n in parts:
                        ins = mm(o, z, w[:, ds(col + c0, n)], start=st, stop=sp_)
                ins.then_inc(h13_mm, 1)

            def hT(g, i, first=False):
                pe.wait_ge(h_ok, g + 1)
                if not first:
                    pe.wait_ge(hTl_ok, g - 1)
                for j in range(3):
                    ins = nc.tensor.transpose(psh[i % 2][:, j * P:(j + 1) * P], hsl[:, i % 2, j * KC:(j + 1) * KC], ident[:, :])
                ins.then_inc(hT_mm, 1)

            def y(g, i, e, first=False):
                pe.wait_ge(hTl_ok, g + 1)
                if not first:
                    pe.wait_ge(y_ev, g)
                b = i % 2
                for j, k in enumerate(KJ):
                    a = ds(e * (3 * C) + j * C, C)
                    hh, hl = hTh[0:k, b, j * P:(j + 1) * P], hTl[0:k, b, j * P:(j + 1) * P]
                    mm(psy, hh, w2h[0:k, a], start=(j == 0), stop=False)
                    mm(psy, hh, w2l[0:k, a], start=False, stop=False)
                    ins = mm(psy, hl, w2h[0:k, a], start=False, stop=(j == 2))
                ins.then_inc(y_mm, 1)

            def expert(g):
                return pe.value_load(etab[0:1, ds(g, 1)], min_val=0, max_val=E - 1)

            zT(0, 0, 16, True)
            for g in range(RING):
                zT(g + 1, (g + 1) % RING, 16 * ((g + 1) // RING + 1))
                h13(g, g, expert(g), g < 2)
                if g >= 1:
                    hT(g - 1, g - 1, g < 3)
                if g >= 2:
                    y(g - 2, g - 2, expert(g - 2), g == 2)
            with pe.Fori(1, NS // RING - 1) as r:
                for i in range(RING):
                    g = r * RING + i
                    zT(g + 1, (i + 1) % RING, r * 16 + (16 if i < RING - 1 else 32))
                    h13(g, i, expert(g))
                    hT(g - 1, i - 1)
                    y(g - 2, i - 2, expert(g - 2))
            for i in range(RING + 2):
                g = NS - RING + i
                if i < RING - 1:
                    zT(g + 1, i + 1, 16 * (NS // RING))
                if i < RING:
                    h13(g, i, expert(g))
                if i < RING + 1:
                    hT(g - 1, i - 1)
                y(g - 2, i - 2, expert(g - 2))


def kernel(x, adj, L0_gnn_W1, L0_gnn_b1, L0_gnn_g1, L0_gnn_be1, L0_gnn_W2, L0_gnn_b2, L0_gnn_g2, L0_gnn_be2,
           L0_ffn_router_w, L0_ffn_w1, L0_ffn_w2, L0_ffn_w3):
    import numpy as np
    import concourse.bacc as bacc
    from concourse import mybir
    from concourse.bass_utils import run_bass_kernel_spmd as run

    c = np.ascontiguousarray
    a = lambda v: np.asarray(v)
    cols = lambda v: a(v).reshape(-1, P).T
    w13 = np.concatenate([a(L0_ffn_w1), a(L0_ffn_w3)], axis=1)
    arrays = {
        "x_rows": c(a(x).reshape(TOK, C)),
        "adj_in": c(a(adj)),
        "gnn_w1_t": c(a(L0_gnn_W1).T),
        "gnn_w2_t": c(a(L0_gnn_W2).T),
        "gnn_vectors": c(np.concatenate([cols(L0_gnn_b1), cols(L0_gnn_g1), cols(L0_gnn_be1), cols(L0_gnn_b2),
                                         cols(L0_gnn_g2), cols(L0_gnn_be2)], axis=1)),
        "router_t": c(a(L0_ffn_router_w).T),
        "w13_t": c(w13.transpose(2, 0, 1).reshape(C, E * 2 * HF)),
        "w2_t": c(a(L0_ffn_w2).transpose(0, 2, 1).reshape(E * HF, C)),
    }
    nc = bacc.Bacc("TRN2", target_bir_lowering=False, num_devices=1)
    args = [nc.dram_tensor(k, v.shape, mybir.dt.from_np(v.dtype), kind="ExternalInput").ap() for k, v in arrays.items()]
    out = nc.dram_tensor("out_rows", (TOK, C), mybir.dt.float32, kind="ExternalOutput").ap()
    build(nc, *args, out)
    got = run(nc, [arrays], core_ids=[0])
    return got.results[0]["out_rows"].reshape(B, N, C)
```

```python
import concourse.bass as bass
from concourse import mybir
from contextlib import ExitStack

P = 128
B, N, C = 128, 64, 128
TOK = B * N
T = TOK // P
GT = 4
GR = T // GT
GC = GT * P
QT = T // 4
HID = 256
HALVES = HID // P
E, TOPK, HF = 8, 2, 341
EPS = 1e-5
CHUNKS = (16, 32, 16)
RING = 8
UNIT = 2
UNITS = RING // UNIT
SLOTS = tuple(-(-(TOPK * nt + E - 1) // RING) * RING for nt in CHUNKS)
NS = sum(SLOTS)
ROW = C + 1
HA = 342
HB = 2 * HF - HA
PAD = 512 - HA
KC = 114
KJ = (KC, KC, HF - 2 * KC)


def build(nc, x, adj, gw1, gw2, gvec, rw, w13, w2, out):
    f32, f32r, i32 = mybir.dt.float32, mybir.dt.float32r, mybir.dt.int32
    ACT, ALU, AX = mybir.ActivationFunctionType, mybir.AluOpType, mybir.AxisListType.X
    ds = bass.ds
    V, S = nc.vector, nc.scalar
    chunk0 = [sum(CHUNKS[:c]) for c in range(len(CHUNKS))]
    slot0 = [sum(SLOTS[:c]) for c in range(len(CHUNKS))]
    NTX, NSX = max(CHUNKS), max(SLOTS)

    sent = [nc.dram_tensor(f"sent{c}", [s * P, ROW], f32, kind="Internal").ap() for c, s in enumerate(SLOTS)]
    back = [nc.dram_tensor(f"back{c}", [s * P, C], f32, kind="Internal").ap() for c, s in enumerate(SLOTS)]

    with ExitStack() as ctx:
        def sb(name, shape, dt=f32):
            return ctx.enter_context(nc.sbuf_tensor(name, shape, dt))

        def sem(name):
            return ctx.enter_context(nc.semaphore(name))

        xs = sb("xs", [P, T, C])
        big = sb("big", [P, 2 * TOK + T])
        hid = [big[:, h * TOK:(h + 1) * TOK] for h in range(HALVES)]
        gout = hid[0]
        zrow = big[:, TOK:TOK + T * ROW].rearrange("p (t r) -> p t r", r=ROW)
        w13s = sb("w13s", [P, E * 2 * 2 * HF], f32r)
        w2s = sb("w2s", [KC, E * 3 * 2 * C], f32r)
        zTh, zTl = sb("zTh", [P, 2, P], f32r), sb("zTl", [P, 2, P], f32r)
        hTh, hTl = sb("hTh", [KC, 2, 3 * P], f32r), sb("hTl", [KC, 2, 3 * P], f32r)

        arena = sb("arena", [P, 2 * QT * C + 2 * GC + 2 * HF + 3 * C + 64])
        at = [0]

        def part(n):
            at[0] += n
            return arena[:, at[0] - n:at[0]]

        fring = part(2 * QT * C).rearrange("p (t c) -> p t c", c=C)
        aggT = part(2 * GC).rearrange("p (b n) -> p b n", b=2)
        st13 = part(2 * HF)
        st2 = part(3 * C)
        at[0] = 0
        zslot = part(RING * ROW).rearrange("p (s r) -> p s r", r=ROW)
        sil = part(2 * HF).rearrange("p (b n) -> p b n", b=2)
        hsl = part(2 * 3 * KC).rearrange("p (b n) -> p b n", b=2)
        ysl = part(RING * C).rearrange("p (s c) -> p s c", c=C)
        zTr = part(2 * GC).rearrange("p (b n) -> p b n", b=2)
        first = part(E * NTX)
        ran = part(E * NTX + 1)
        tmp = [first, ran[:, 1:]] + [part(E * NTX) for _ in range(5)]
        so_e, slot_cmp = first[0:1, 0:NSX], arena[0:1, at[0] - 5 * E * NTX:at[0]]

        ident, ones = sb("ident", [P, P]), sb("ones", [P, P])
        blk, ahat = sb("blk", [P, P]), sb("ahat", [P, P])
        gw1s, gw2s = sb("gw1s", [P, HID]), sb("gw2s", [P, HALVES, C])
        vec, rws = sb("vec", [P, 9]), sb("rws", [P, E])
        b1, g1, be1 = vec[:, 0:2], vec[:, 2:4], vec[:, 4:6]
        b2, g2, be2 = vec[:, 6:7], vec[:, 7:8], vec[:, 8:9]
        zero = sb("zero", [P, ROW])
        st6 = sb("st6", [P, T, 6])
        hst = sb("hst", [P, HALVES, GR * 6])
        ost = sb("ost", [P, GR * 6])
        mean, rstd, nmr = sb("mean", [P, T]), sb("rstd", [P, T]), sb("nmr", [P, T])
        rv, rs, rt = sb("rv", [P, T]), sb("rs", [P, T]), sb("rt", [P, T])
        mv = sb("mv", [P, HALVES, 2])
        bnsc, bnsh = sb("bnsc", [P, 3]), sb("bnsh", [P, 3])
        deg = sb("deg", [P, 4])
        revi, rev = sb("revi", [P, E], i32), sb("rev", [P, E])
        so = sb("so", [1, NSX])
        gate2 = sb("gate2", [P, T])
        idx = [sb(f"idx{k}", [P, T], i32) for k in range(TOPK)]
        etab = sb("etab", [1, NS], i32)
        soi = etab[:, 0:NSX]
        sm = sb("sm", [P, 6, NTX])
        cnt = sb("cnt", [P, 4, E])
        cnti = sb("cnti", [P, 2, E], i32)
        before = sb("before", [P, P])

        ps = ctx.enter_context(nc.psum_tensor("ps", [P, 8, 512], f32))
        psA = [ps[:, b, :] for b in (0, 1)]
        psH = [ps[:, 2 + 2 * b:4 + 2 * b, :] for b in (0, 1)]
        psT = [ps[:, b, :] for b in (2, 3)]
        psZ = [ps[:, b, :] for b in (4, 5)]
        psL = [ps[:, b, :] for b in (6, 7)]
        psR = ps[:, 0, :]
        flat = ps[:, :, :].rearrange("p b n -> p (b n)")
        ps13 = [flat[:, 1024 * b + PAD:1024 * b + PAD + 2 * HF] for b in (0, 1)]
        psz = ps[:, 4, 0:P]
        psh = [ps[0:KC, 5 + b, 0:3 * P] for b in (0, 1)]
        psy = ps[:, 7, 0:2 * C]

        x_in = [sem(f"x_in{q}") for q in range(4)]
        adj_in, par_in = sem("adj_in"), sem("par_in")
        stage13_in, stage2_in = sem("stage13_in"), sem("stage2_in")
        zeroed = sem("zeroed")
        consts, cleared = sem("consts"), sem("cleared")
        split = sem("split")
        stat_ok = sem("stat_ok")
        dseq = sem("dseq")
        root_in, root_out = sem("root_in"), sem("root_out")
        adj_col, adj_sc, adj_T, adj_ok = sem("adj_col"), sem("adj_sc"), sem("adj_T"), sem("adj_ok")
        nmr_ok, f_act = sem("nmr_ok"), sem("f_act")
        f_ready, agg_mm, agg_ev = sem("f_ready"), sem("agg_mm"), sem("agg_ev")
        hid_mm, hid_ev = sem("hid_mm"), sem("hid_ev")
        bn1_ok, bn2_ok, relu_ok = sem("bn1_ok"), sem("bn2_ok"), sem("relu_ok")
        out_mm, out_ev, ostat = sem("out_mm"), sem("out_ev"), sem("ostat")
        bnout, outT_mm, x2_ok = sem("bnout"), sem("outT_mm"), sem("x2_ok")
        z_ok, zr_mm, zr_ev, logit_mm = sem("z_ok"), sem("zr_mm"), sem("zr_ev"), sem("logit_mm")
        ex_in, ex_out = sem("ex_in"), sem("ex_out")
        v2_ok, sel_ok, rank_mm = sem("v2_ok"), sem("sel_ok"), sem("rank_mm")
        routed, etab_ok = sem("routed"), sem("etab_ok")
        sent_k = [sem(f"sent_k{k}") for k in range(TOPK)]
        regate = sem("regate")
        slot_in = [sem(f"slot_in{u}") for u in range(UNITS)]
        slot_out = [sem(f"slot_out{u}") for u in range(UNITS)]
        zT_mm, zh_ok, zl_ok = sem("zT_mm"), sem("zh_ok"), sem("zl_ok")
        h13_mm, silu_ok, h_ok = sem("h13_mm"), sem("silu_ok"), sem("h_ok")
        hT_mm, hTh_ok, hTl_ok = sem("hT_mm"), sem("hTh_ok"), sem("hTl_ok")
        y_mm, y_lo, y_ev = sem("y_mm"), sem("y_lo"), sem("y_ev")
        got_k = [sem(f"got_k{k}") for k in range(TOPK)]
        stored = sem("stored")

        block = ctx.enter_context(nc.Block())

        @block.sync
        def _(sp):
            xv = x.rearrange("(t p) c -> p t c", p=P)

            def load_x(q):
                sp.dma_start(xs[:, q * QT:(q + 1) * QT, :], xv[:, q * QT:(q + 1) * QT, :]).then_inc(x_in[q], 16)

            sp.dma_start(blk[0:N, 0:N], adj).then_inc(adj_in, 16)
            sp.dma_start(blk[N:P, N:P], adj).then_inc(adj_in, 16)
            load_x(0)
            sp.dma_start(gw1s[:, :], gw1).then_inc(par_in, 16)
            sp.dma_start(vec[:, :], gvec).then_inc(par_in, 16)
            for q in range(1, 4):
                load_x(q)
            sp.dma_start(gw2s[:, :, :], gw2.rearrange("(h p) o -> p h o", p=P)).then_inc(par_in, 16)
            sp.dma_start(rws[:, :], rw).then_inc(par_in, 16)
            with sp.Fori(0, E) as e:
                sp.wait_ge(split, e * 4 + 1)
                sp.dma_start(st13, w13[:, ds(e * (2 * HF), 2 * HF)]).then_inc(stage13_in, 16)
                sp.dma_start(st2[0:KC, :].rearrange("p (j c) -> p j c", j=3)[:, 0:2, :],
                             w2[ds(e * HF, 2 * KC), :].rearrange("(j p) c -> p j c", p=KC)).then_inc(stage2_in, 16)
                sp.dma_start(st2[0:KJ[2], 2 * C:3 * C], w2[ds(e * HF + 2 * KC, KJ[2]), :]).then_inc(stage2_in, 16)

            def step(src, u, src_row, dst, dst_row, done):
                if done is not None:
                    sp.wait_ge(y_ev, done)
                if dst is not None:
                    sp.dma_start(dst[ds(dst_row, UNIT * P), :].rearrange("(s p) c -> p s c", p=P),
                                 ysl[:, UNIT * u:UNIT * u + UNIT, :]).then_inc(slot_out[u], 16)
                if src is not None:
                    sp.dma_start(zslot[:, UNIT * u:UNIT * u + UNIT, :],
                                 src[ds(src_row, UNIT * P), :].rearrange("(s p) c -> p s c", p=P)).then_inc(slot_in[u], 16)

            for c in range(len(CHUNKS)):
                for k in range(TOPK):
                    sp.wait_ge(sent_k[k], 16 * (chunk0[c] + CHUNKS[c]))
                for u in range(UNITS):
                    n = slot0[c] // UNIT + u
                    step(sent[c], u, u * UNIT * P,
                         back[c - 1] if c else None, (SLOTS[c - 1] - RING + u * UNIT) * P if c else None,
                         UNIT * (n - UNITS + 1) if c else None)
                with sp.Fori(1, SLOTS[c] // RING) as r:
                    for u in range(UNITS):
                        step(sent[c], u, r * (RING * P) + u * UNIT * P,
                             back[c], r * (RING * P) + (u * UNIT - RING) * P,
                             r * RING + (slot0[c] + u * UNIT - RING + UNIT))
            for u in range(UNITS):
                step(None, u, None, back[-1], (SLOTS[-1] - RING + u * UNIT) * P, NS - RING + (u + 1) * UNIT)

        @block.gpsimd
        def _(gp):
            gp.memset(blk[0:N, N:P], 0.0).then_inc(cleared, 1)
            gp.memset(blk[N:P, 0:N], 0.0).then_inc(cleared, 1)
            gp.wait_ge(cleared, 2)
            gp.memset(st2, 0.0).then_inc(split, 1)
            gp.memset(zero[:, :], 0.0).then_inc(consts, 1)
            gp.memset(ident[:, :], 0.0).then_inc(consts, 1)
            gp.memset(ones[:, :], 1.0).then_inc(consts, 1)
            gp.iota(revi[:, :], [[-1, E]], base=E, channel_multiplier=0).then_inc(consts, 1)
            gp.iota(soi, [[1, NSX]], base=0, channel_multiplier=0).then_inc(consts, 1)
            gp.wait_ge(consts, 5)
            gp.affine_select(out=ident[:, :], in_=ident[:, :], compare_op=ALU.not_equal, fill=1.0,
                             base=0, pattern=[[-1, P]], channel_multiplier=1).then_inc(consts, 1)
            gp.affine_select(out=before[:, :], in_=zero[:, 0:P], compare_op=ALU.is_gt, fill=-1.0,
                             base=0, pattern=[[1, P]], channel_multiplier=-1).then_inc(consts, 1)
            gp.tensor_copy(rev[:, :], revi[:, :]).then_inc(consts, 1)
            gp.tensor_copy(so[:, :], soi).then_inc(consts, 1)
            gp.wait_ge(x_in[3], 16)
            for c, s in enumerate(SLOTS):
                gp.dma_start(sent[c].rearrange("(p s) r -> p s r", p=P),
                             zero[:, :].unsqueeze(1).broadcast_to([P, s, ROW])).then_inc(zeroed, 16)
            with gp.Fori(0, E) as e:
                gp.wait_ge(stage13_in, e * 16 + 16)
                hi, lo = ds(e * (4 * HF), 2 * HF), ds(e * (4 * HF) + 2 * HF, 2 * HF)
                gp.tensor_copy(w13s[:, hi], st13).then_inc(split, 1)
                gp.wait_ge(split, e * 4 + 2)
                gp.tensor_tensor(w13s[:, lo], st13, w13s[:, hi].bitcast(f32), ALU.subtract).then_inc(split, 1)
                gp.wait_ge(stage2_in, e * 32 + 32)
                parts = w2s[:, ds(e * (6 * C), 6 * C)].rearrange("p (j b c) -> p j b c", j=3, b=2)
                raw = st2[0:KC, :].rearrange("p (j c) -> p j c", j=3)
                gp.tensor_copy(parts[:, :, 0, :], raw).then_inc(split, 1)
                gp.wait_ge(split, e * 4 + 4)
                gp.tensor_tensor(parts[:, :, 1, :], raw, parts[:, :, 0, :].bitcast(f32), ALU.subtract).then_inc(split, 1)
            gp.wait_ge(zeroed, 16 * len(CHUNKS))
            for c, nt in enumerate(CHUNKS):
                gp.wait_ge(routed, c + 1)
                tiles = slice(chunk0[c], chunk0[c] + nt)
                for k in range(TOPK):
                    if k:
                        gp.wait_ge(sent_k[0], 16 * (chunk0[c] + nt))
                        gp.tensor_copy(zrow[:, tiles, C], gate2[:, tiles]).then_inc(regate, 1)
                        gp.wait_ge(regate, c + 1)
                    for t in range(chunk0[c], chunk0[c] + nt):
                        gp.indirect_dma_start(sent[c], bass.IndirectOffsetOnAxis(idx[k][:, t:t + 1], 0),
                                              zrow[:, t, :], None).then_inc(sent_k[k], 16)
            ov = out.rearrange("(t p) c -> p t c", p=P)
            for c, nt in enumerate(CHUNKS):
                tiles = slice(chunk0[c], chunk0[c] + nt)
                for u in range(UNITS):
                    gp.wait_ge(slot_out[u], 16 * ((slot0[c] + SLOTS[c]) // RING))
                for k in range(TOPK):
                    for t in range(chunk0[c], chunk0[c] + nt):
                        gp.indirect_dma_start(xs[:, t, :], None, back[c],
                                              bass.IndirectOffsetOnAxis(idx[k][:, t:t + 1], 0),
                                              compute_op=ALU.add).then_inc(got_k[k], 16)
                    gp.wait_ge(got_k[k], 16 * (chunk0[c] + nt))
                gp.dma_start(ov[:, tiles, :], xs[:, tiles, :]).then_inc(stored, 16)
            gp.wait_ge(stored, 16 * len(CHUNKS))

        @block.scalar
        def _(act):
            roots = [0]

            def root(cols):
                roots[0] += 1
                act.wait_ge(root_in, roots[0])
                S.activation(rs[:, cols], rv[:, cols], ACT.Sqrt).then_inc(root_out, 1)

            root(slice(0, 1))

            def ln_tile(g):
                if g >= 2 * QT // GT:
                    act.wait_ge(agg_mm, g - 2 * QT // GT + 1)
                t = g * GT + GT - 1
                S.activation(fring[:, t % (2 * QT), :], xs[:, t, :], ACT.Identity,
                             bias=nmr[:, t:t + 1], scale=rstd[:, t:t + 1]).then_inc(f_act, 1)

            def agg_out(g, b, first=False):
                act.wait_ge(agg_mm, g + 1)
                if not first:
                    act.wait_ge(hid_mm, g * 2 - 2)
                S.activation(aggT[:, b, :], psA[b], ACT.Copy).then_inc(agg_ev, 1)

            def hid_out(g, b):
                for h in range(HALVES):
                    act.wait_ge(hid_mm, g * 2 + (h + 1))
                    S.activation(hid[h][:, ds(g * GC, GC)], psH[b][:, h, :], ACT.Identity,
                                 bias=b1[:, h:h + 1]).then_inc(hid_ev, 1)

            G1 = QT // GT
            root(slice(0, QT))
            act.wait_ge(nmr_ok, 1)
            for g in range(G1):
                ln_tile(g)
            act.wait_ge(par_in, 64)
            for g in range(GR):
                if g == G1 - 1:
                    root(slice(QT, T))
                    act.wait_ge(nmr_ok, 2)
                    ln_tile(g + 1)
                    ln_tile(g + 2)
                if g == 0:
                    agg_out(0, 0, True)
                if g + 1 < GR:
                    agg_out(g + 1, (g + 1) % 2, g == 0)
                hid_out(g, g % 2)
                if G1 - 1 <= g < GR - 3:
                    ln_tile(g + 3)
            root(slice(0, 2))
            act.wait_ge(bn1_ok, 1)
            with act.Fori(0, GR) as g:
                for h in range(HALVES):
                    S.activation(hid[h][:, ds(g * GC, GC)], hid[h][:, ds(g * GC, GC)], ACT.Relu,
                                 bias=bnsh[:, h:h + 1], scale=bnsc[:, h:h + 1]).then_inc(relu_ok, 1)
            root(slice(0, 1))
            act.wait_ge(bn2_ok, 1)

            def bn_apply(c):
                with act.Fori(chunk0[c] // GT, (chunk0[c] + CHUNKS[c]) // GT) as g:
                    a = gout[:, ds(g * GC, GC)]
                    S.activation(a, a, ACT.Identity, bias=bnsh[:, 2:3], scale=bnsc[:, 2:3]).then_inc(bnout, 1)

            def zr_out(g):
                act.wait_ge(zr_mm, g + 1)
                if g >= 2:
                    act.wait_ge(logit_mm, g - 1)
                S.activation(zTr[:, g % 2, :], psZ[g % 2], ACT.Copy).then_inc(zr_ev, 1)

            def scales(c):
                root(slice(chunk0[c], chunk0[c] + CHUNKS[c]))

            bn_apply(0)
            bn_apply(1)
            scales(0)
            for c, nt in enumerate(CHUNKS):
                g0, g1 = chunk0[c] // GT, (chunk0[c] + nt) // GT
                act.wait_ge(nmr_ok, 2 + c + 1)
                for g in range(g0, g1):
                    for t in range(g * GT, (g + 1) * GT):
                        ins = S.activation(zrow[:, t, 0:C], xs[:, t, :], ACT.Identity,
                                           bias=nmr[:, t:t + 1], scale=rstd[:, t:t + 1])
                    ins.then_inc(z_ok, 1)
                    if g > g0:
                        zr_out(g - 1)
                    if g == g0 + 3 and c + 1 < len(CHUNKS):
                        scales(c + 1)
                zr_out(g1 - 1)
                if c + 2 < len(CHUNKS):
                    bn_apply(c + 2)
                act.wait_ge(ex_in, c + 1)
                S.activation(tmp[1][:, 0:E * nt], tmp[0][:, 0:E * nt], ACT.Exp).then_inc(ex_out, 1)
                act.wait_ge(v2_ok, c + 1)
                S.activation(sm[:, 3, 0:nt], sm[:, 2, 0:nt], ACT.Exp).then_inc(ex_out, 1)

            def z_hi(g, i):
                act.wait_ge(zT_mm, g + 1)
                S.activation(zTh[:, i % 2, :], psz, ACT.Copy).then_inc(zh_ok, 1)

            def silu(g, i):
                act.wait_ge(h13_mm, g + 1)
                S.activation(sil[:, i % 2, :], ps13[i % 2][:, 0:HF], ACT.Silu).then_inc(silu_ok, 1)

            def hT_hi(g, i):
                act.wait_ge(hT_mm, g + 1)
                S.activation(hTh[:, i % 2, :], psh[i % 2], ACT.Copy).then_inc(hTh_ok, 1)

            def y_low(g, i, used):
                act.wait_ge(y_mm, g + 1)
                if used is not None and i % UNIT == 0:
                    act.wait_ge(slot_out[i // UNIT], used)
                S.activation(ysl[:, i, :], psy[:, C:2 * C], ACT.Copy, scale=zslot[:, i, C:ROW]).then_inc(y_lo, 1)

            z_hi(0, 0)
            for g in range(2 * RING):
                z_hi(g + 1, g + 1)
                silu(g, g)
                if g >= 1:
                    hT_hi(g - 1, g - 1)
                if g >= 2:
                    y_low(g - 2, (g - 2) % RING, 16 if g - 2 >= RING else None)
            with act.Fori(2, NS // RING - 1) as r:
                for i in range(RING):
                    g = r * RING + i
                    z_hi(g + 1, i + 1)
                    silu(g, i)
                    hT_hi(g - 1, i - 1)
                    y_low(g - 2, (i - 2) % RING, r * 16 if i >= 2 else r * 16 - 16)
            for i in range(RING + 2):
                g = NS - RING + i
                if i < RING - 1:
                    z_hi(g + 1, i + 1)
                if i < RING:
                    silu(g, i)
                if i < RING + 1:
                    hT_hi(g - 1, i - 1)
                y_low(g - 2, (i - 2) % RING, 16 * ((g - 2) // RING))

        @block.vector
        def _(dve):
            seq, roots, seen = [0], [0], [0]

            def link(ins):
                seq[0] += 1
                ins.then_inc(dseq, 1)
                dve.wait_ge(dseq, seq[0])

            def stats(groups):
                seen[0] += groups
                dve.wait_ge(stat_ok, seen[0])

            def rsqrt(dst, cols):
                roots[0] += 1
                a = rv[:, cols]
                dve.wait_ge(root_out, roots[0])
                link(V.reciprocal(dst, rs[:, cols]))
                link(V.tensor_tensor(rt[:, cols], dst, dst, ALU.mult))
                link(V.tensor_tensor(rt[:, cols], rt[:, cols], a, ALU.mult))
                link(V.tensor_scalar(rt[:, cols], rt[:, cols], -0.5, 1.5, ALU.mult, ALU.add))
                link(V.tensor_tensor(dst, dst, rt[:, cols], ALU.mult))

            dve.wait_ge(consts, 9)
            dve.wait_ge(cleared, 2)
            dve.wait_ge(adj_in, 32)
            link(V.tensor_tensor(blk[:, :], blk[:, :], ident[:, :], ALU.add))
            V.tensor_reduce(deg[:, 0:1], blk[:, :], AX, ALU.add).then_inc(adj_sc, 1)
            link(V.tensor_tensor(ahat[:, :], blk[:, :], ident[:, :], ALU.mult))
            link(V.tensor_reduce(deg[:, 1:2], ahat[:, :], AX, ALU.add))
            link(V.tensor_tensor(deg[:, 2:3], deg[:, 0:1], deg[:, 1:2], ALU.subtract))
            dve.wait_ge(adj_col, 1)
            V.tensor_tensor(rv[:, 0:1], psA[0][:, 0:1], deg[:, 2:3], ALU.add).then_inc(root_in, 1)
            rsqrt(deg[:, 3:4], slice(0, 1))
            V.tensor_scalar(blk[:, :], blk[:, :], deg[:, 3:4], None, ALU.mult).then_inc(adj_sc, 1)
            dve.wait_ge(adj_T, 1)
            V.tensor_scalar(ahat[:, :], psA[1][:, 0:P], deg[:, 3:4], None, ALU.mult).then_inc(adj_ok, 1)

            def ln_stats(t0, n):
                cols = slice(t0, t0 + n)
                s = st6[:, cols, :]
                link(V.tensor_tensor(rs[:, cols], s[:, :, 1], s[:, :, 4], ALU.subtract))
                link(V.tensor_tensor(rt[:, cols], rs[:, cols], rs[:, cols], ALU.mult))
                link(V.tensor_tensor(mean[:, cols], s[:, :, 1], s[:, :, 4], ALU.add))
                link(V.tensor_scalar(mean[:, cols], mean[:, cols], 0.5, None, ALU.mult))
                link(V.tensor_tensor(rv[:, cols], s[:, :, 2], s[:, :, 5], ALU.add))
                link(V.tensor_scalar(rv[:, cols], rv[:, cols], 1.0 / C, EPS, ALU.mult, ALU.add))
                V.scalar_tensor_tensor(rv[:, cols], rt[:, cols], 0.25, rv[:, cols], ALU.mult, ALU.add).then_inc(root_in, 1)

            def ln_scales(t0, n):
                cols = slice(t0, t0 + n)
                ln_stats(t0, n)
                rsqrt(rstd[:, cols], cols)
                V.scalar_tensor_tensor(nmr[:, cols], mean[:, cols], -1.0, rstd[:, cols], ALU.mult, ALU.mult).then_inc(nmr_ok, 1)

            def x_stats(q):
                dve.wait_ge(x_in[q], 16)
                for t in range(q * QT, (q + 1) * QT):
                    ins = V.bn_stats(st6[:, t, :], xs[:, t, :])
                ins.then_inc(stat_ok, 1)

            def ln_group(g):
                if g >= 2 * QT // GT:
                    dve.wait_ge(agg_mm, g - 2 * QT // GT + 1)
                for t in range(g * GT, g * GT + GT - 1):
                    ins = V.tensor_scalar(fring[:, t % (2 * QT), :], xs[:, t, :],
                                          mean[:, t:t + 1], rstd[:, t:t + 1], ALU.subtract, ALU.mult)
                ins.then_inc(f_ready, 1)

            def hid_stats(g):
                for h in range(HALVES):
                    dve.wait_ge(hid_ev, g * 2 + h + 1)
                    ins = V.bn_stats(hst[:, h, g * 6:(g + 1) * 6], hid[h][:, g * GC:(g + 1) * GC])
                ins.then_inc(stat_ok, 1)

            x_stats(0)
            stats(1)
            ln_scales(0, QT)
            for g in range(QT // GT):
                ln_group(g)
            for q in range(1, 4):
                x_stats(q)
            stats(3)
            ln_scales(QT, T - QT)
            for g in range(QT // GT, GR):
                ln_group(g)
                hid_stats(g - QT // GT)
            for g in range(GR - QT // GT, GR):
                hid_stats(g)
            stats(GR)

            def bn_finish(n, gamma, beta, at, done):
                V.tensor_scalar(rv[:, 0:n], mv[:, 0:n, 1], EPS, None, ALU.add).then_inc(root_in, 1)
                rsqrt(rstd[:, 0:n], slice(0, n))
                link(V.tensor_tensor(bnsc[:, at:at + n], rstd[:, 0:n], gamma, ALU.mult))
                link(V.tensor_tensor(rt[:, 0:n], mv[:, 0:n, 0], bnsc[:, at:at + n], ALU.mult))
                V.tensor_tensor(bnsh[:, at:at + n], beta, rt[:, 0:n], ALU.subtract).then_inc(done, 1)

            for h in range(HALVES):
                link(V.bn_aggr(mv[:, h, :], hst[:, h, :]))
            bn_finish(2, g1, be1, 0, bn1_ok)

            def gout_out(g, b):
                dve.wait_ge(out_mm, g + 1)
                a = gout[:, ds(g * GC, GC)]
                V.tensor_scalar(a, psA[b], b2, None, ALU.add).then_inc(out_ev, 1)
                dve.wait_ge(out_ev, g + 1)
                V.bn_stats(ost[:, ds(g * 6, 6)], a).then_inc(stat_ok, 1)

            with dve.Fori(0, GR // 2) as j:
                gout_out(j * 2, 0)
                gout_out(j * 2 + 1, 1)
            stats(GR)
            link(V.bn_aggr(mv[:, 0, :], ost[:, :]))
            bn_finish(1, g2, be2, 2, bn2_ok)

            def residuals(c):
                g0, g1 = chunk0[c] // GT, (chunk0[c] + CHUNKS[c]) // GT
                for g in range(g0, g1):
                    dve.wait_ge(outT_mm, g + 1)
                    a = xs[:, g * GT:(g + 1) * GT, :].rearrange("p t c -> p (t c)")
                    V.tensor_tensor(a, psT[g % 2], a, ALU.add).then_inc(x2_ok, 1)
                    if g > g0:
                        row_stats(g - 1)
                row_stats(g1 - 1)
                stats(1)

            def row_stats(g):
                dve.wait_ge(x2_ok, g + 1)
                for t in range(g * GT, (g + 1) * GT):
                    ins = V.bn_stats(st6[:, t, :], xs[:, t, :])
                if g + 1 in [(chunk0[c] + CHUNKS[c]) // GT for c in range(len(CHUNKS))]:
                    ins.then_inc(stat_ok, 1)

            def route(c):
                t0, nt, ns = chunk0[c], CHUNKS[c], SLOTS[c]
                n = E * nt
                et = lambda a: a.rearrange("p (e t) -> p e t", t=nt)
                te = lambda a: a.rearrange("p (e t) -> p t e", t=nt)
                over_e = lambda a: a.unsqueeze(1).broadcast_to([P, E, nt])
                over_t = lambda a: a.unsqueeze(2).broadcast_to([P, E, nt])
                mx, k1, v2, e2, den, s = (sm[:, i, 0:nt] for i in range(6))
                d, ex, key, m1, m2, both, pf = (a[:, 0:n] for a in tmp[:7])
                dve.wait_ge(logit_mm, (t0 + nt) // GT)
                lg = psL[c % 2][:, 0:n].rearrange("p (t e) -> p t e", e=E)
                link(V.tensor_reduce(mx, lg, AX, ALU.max))
                V.tensor_tensor(et(d), lg.rearrange("p t e -> p e t"), over_e(mx), ALU.subtract).then_inc(ex_in, 1)
                dve.wait_ge(ex_in, c + 1)
                link(V.scalar_tensor_tensor(et(key), et(d), 0.0, over_t(rev[:, :]), ALU.is_equal, ALU.mult))
                link(V.tensor_reduce(k1, te(key), AX, ALU.max))
                link(V.tensor_tensor(et(m1), over_t(rev[:, :]), over_e(k1), ALU.is_equal))
                link(V.scalar_tensor_tensor(pf, m1, -1e30, d, ALU.mult, ALU.add))
                V.tensor_reduce(v2, te(pf), AX, ALU.max).then_inc(v2_ok, 1)
                dve.wait_ge(v2_ok, c + 1)
                link(V.tensor_tensor(et(key), et(pf), over_e(v2), ALU.is_equal))
                link(V.tensor_tensor(et(key), et(key), over_t(rev[:, :]), ALU.mult))
                link(V.tensor_reduce(k1, te(key), AX, ALU.max))
                link(V.tensor_tensor(et(m2), over_t(rev[:, :]), over_e(k1), ALU.is_equal))
                V.tensor_tensor(both, m1, m2, ALU.add).then_inc(sel_ok, 1)
                dve.wait_ge(ex_out, 2 * c + 2)
                link(V.tensor_reduce(s, te(ex), AX, ALU.add))
                link(V.scalar_tensor_tensor(den, s, 1e-9, e2, ALU.mult, ALU.add))
                link(V.tensor_scalar(den, den, 1.0, None, ALU.add))
                link(V.reciprocal(den, den))
                link(V.tensor_scalar(zrow[:, t0:t0 + nt, C], den, 1.0, None, ALU.mult))
                link(V.tensor_tensor(gate2[:, t0:t0 + nt], e2, den, ALU.mult))
                rank, tot = psR[:, 0:n], psR[:, n:2 * n]
                cn, cum, off = (cnt[:, i, :] for i in range(3))
                ends = ran[:, 1:n + 1].rearrange("p (e t) -> p e t", t=nt)[:, :, nt - 1]
                starts = ran[:, 0:n].rearrange("p (e t) -> p e t", t=nt)[:, :, 0]
                dve.wait_ge(rank_mm, c + 1)
                link(V.tensor_tensor_scan(ran[:, 1:n + 1], ones[:, 0:1].broadcast_to([P, n]), tot, 0.0, ALU.mult, ALU.add))
                link(V.tensor_tensor(cn, ends, starts, ALU.subtract))
                link(V.tensor_scalar(cnti[:, 0, :], cn, float(P - 1), None, ALU.add))
                link(V.tensor_scalar(cnti[:, 1, :], cnti[:, 0, :], P.bit_length() - 1, None, ALU.arith_shift_right))
                link(V.tensor_tensor_scan(cum, ones[:, 0:E], cnti[:, 1, :], 0.0, ALU.mult, ALU.add))
                link(V.tensor_tensor(off, cum, cnti[:, 1, :], ALU.subtract))
                link(V.scalar_tensor_tensor(off, off, float(P), starts, ALU.mult, ALU.subtract))
                link(V.tensor_tensor(pf, rank, ran[:, 1:n + 1], ALU.add))
                link(V.tensor_tensor(et(pf), et(pf), over_t(off), ALU.add))
                with nc.allow_low_precision(reason="places are whole numbers below 2**24"):
                    for k, m in enumerate((m1, m2)):
                        link(V.tensor_tensor(key, m, pf, ALU.mult))
                        ins = V.tensor_reduce(idx[k][:, t0:t0 + nt], te(key), AX, ALU.add)
                        if k:
                            ins.then_inc(routed, 1)
                        else:
                            link(ins)
                dve.wait_ge(routed, c + 1)
                cmp = slot_cmp[:, 0:E * ns].rearrange("p (s e) -> p s e", e=E)
                link(V.tensor_tensor(cmp, so[0:1, 0:ns].unsqueeze(2).broadcast_to([1, ns, E]),
                                     cum[0:1, :].unsqueeze(1).broadcast_to([1, ns, E]), ALU.is_ge))
                link(V.tensor_reduce(so_e[:, 0:ns], cmp, AX, ALU.add))
                V.tensor_scalar(etab[0:1, slot0[c]:slot0[c] + ns], so_e[:, 0:ns], float(E - 1), None, ALU.min).then_inc(etab_ok, 1)

            dve.wait_ge(split, 4 * E + 1)
            link(V.memset(ran[:, 0:1], 0.0))
            residuals(0)
            ln_scales(0, CHUNKS[0])
            for c in range(len(CHUNKS)):
                if c + 1 < len(CHUNKS):
                    residuals(c + 1)
                    ln_scales(chunk0[c + 1], CHUNKS[c + 1])
                route(c)
            dve.wait_ge(etab_ok, len(CHUNKS))
            link(V.memset(hsl[:, :, HF:3 * KC], 0.0))

            def z_lo(g, i):
                dve.wait_ge(zh_ok, g + 1)
                V.tensor_tensor(zTl[:, i % 2, :], psz, zTh[:, i % 2, :].bitcast(f32), ALU.subtract).then_inc(zl_ok, 1)

            def gated(g, i):
                dve.wait_ge(silu_ok, g + 1)
                V.tensor_tensor(hsl[:, i % 2, 0:HF], ps13[i % 2][:, HF:2 * HF], sil[:, i % 2, :], ALU.mult).then_inc(h_ok, 1)

            def hT_lo(g, i):
                dve.wait_ge(hTh_ok, g + 1)
                V.tensor_tensor(hTl[:, i % 2, :], psh[i % 2], hTh[:, i % 2, :].bitcast(f32), ALU.subtract).then_inc(hTl_ok, 1)

            def y_out(g, i):
                dve.wait_ge(y_lo, g + 1)
                V.scalar_tensor_tensor(ysl[:, i, :], psy[:, 0:C], zslot[:, i, C:ROW], ysl[:, i, :],
                                       ALU.mult, ALU.add).then_inc(y_ev, 1)

            z_lo(0, 0)
            for g in range(RING):
                z_lo(g + 1, g + 1)
                gated(g, g)
                if g >= 1:
                    hT_lo(g - 1, g - 1)
                if g >= 2:
                    y_out(g - 2, g - 2)
            with dve.Fori(1, NS // RING - 1) as r:
                for i in range(RING):
                    g = r * RING + i
                    z_lo(g + 1, i + 1)
                    gated(g, i)
                    hT_lo(g - 1, i - 1)
                    y_out(g - 2, (i - 2) % RING)
            for i in range(RING + 2):
                g = NS - RING + i
                if i < RING - 1:
                    z_lo(g + 1, i + 1)
                if i < RING:
                    gated(g, i)
                if i < RING + 1:
                    hT_lo(g - 1, i - 1)
                y_out(g - 2, (i - 2) % RING)

        @block.tensor
        def _(pe):
            mm = nc.tensor.matmul
            dve_sc = [0]
            pe.wait_ge(adj_sc, 1)
            mm(psA[0][:, 0:1], blk[:, :], ones[:, 0:1], start=True, stop=True).then_inc(adj_col, 1)
            pe.wait_ge(adj_sc, 2)
            nc.tensor.transpose(psA[1][:, 0:P], blk[:, :], ident[:, :]).then_inc(adj_T, 1)
            pe.wait_ge(adj_ok, 1)
            pe.wait_ge(par_in, 64)

            def agg(g, b, ring, first=False):
                pe.wait_ge(f_ready, g + 1)
                pe.wait_ge(f_act, g + 1)
                if not first:
                    pe.wait_ge(agg_ev, g - 1)
                for u in range(GT):
                    ins = mm(psA[b][:, u * P:(u + 1) * P], fring[:, ring + u, :], ahat[:, :], start=True, stop=True)
                ins.then_inc(agg_mm, 1)

            def hidden(g, b, first=False):
                pe.wait_ge(agg_ev, g + 1)
                if not first:
                    pe.wait_ge(hid_ev, g * 2 - 2)
                for h in range(HALVES):
                    mm(psH[b][:, h, :], gw1s[:, h * P:(h + 1) * P], aggT[:, b, :], start=True, stop=True).then_inc(hid_mm, 1)

            agg(0, 0, 0, True)
            for g in range(GR):
                if g + 1 < GR:
                    agg(g + 1, (g + 1) % 2, (g + 1) * GT % (2 * QT), g == 0)
                hidden(g, g % 2, g < 2)

            def graph_out(g, b):
                pe.wait_ge(out_ev, g - 1)
                for h in range(HALVES):
                    pe.wait_ge(relu_ok, g * 2 + (h + 1))
                    ins = mm(psA[b], gw2s[:, h, :], hid[h][:, ds(g * GC, GC)], start=(h == 0), stop=(h == HALVES - 1))
                ins.then_inc(out_mm, 1)

            for g in range(2):
                pe.wait_ge(relu_ok, 2 * g + 2)
                for h in range(HALVES):
                    ins = mm(psA[g], gw2s[:, h, :], hid[h][:, g * GC:(g + 1) * GC], start=(h == 0), stop=(h == HALVES - 1))
                ins.then_inc(out_mm, 1)
            with pe.Fori(1, GR // 2) as j:
                graph_out(j * 2, 0)
                graph_out(j * 2 + 1, 1)

            def back_to_rows(g, b, first=False):
                pe.wait_ge(bnout, g + 1)
                if not first:
                    pe.wait_ge(x2_ok, g - 1)
                for u in range(GT):
                    ins = nc.tensor.transpose(psT[b][:, u * P:(u + 1) * P], gout[:, ds(g * GC + u * P, P)], ident[:, :])
                ins.then_inc(outT_mm, 1)

            def z_cols(g, b, first=False):
                pe.wait_ge(z_ok, g + 1)
                if not first:
                    pe.wait_ge(zr_ev, g - 1)
                for u in range(GT):
                    ins = nc.tensor.transpose(psZ[b][:, u * P:(u + 1) * P], zrow[:, g * GT + u, 0:C], ident[:, :])
                ins.then_inc(zr_mm, 1)

            def logits(g, b, c):
                pe.wait_ge(zr_ev, g + 1)
                for u in range(GT):
                    ins = mm(psL[c % 2][:, ds((g * GT + (u - chunk0[c])) * E, E)], zTr[:, b, u * P:(u + 1) * P],
                             rws[:, :], start=True, stop=True)
                ins.then_inc(logit_mm, 1)

            def rows(c):
                g0 = chunk0[c] // GT
                ng = CHUNKS[c] // GT
                for g in range(g0, g0 + ng):
                    back_to_rows(g, g % 2, g < 2)

            def ranks(c):
                n = E * CHUNKS[c]
                pe.wait_ge(sel_ok, c + 1)
                if c:
                    pe.wait_ge(routed, c)
                mm(psR[:, 0:n], before[:, :], tmp[5][:, 0:n], start=True, stop=True)
                mm(psR[:, n:2 * n], ones[:, :], tmp[5][:, 0:n], start=True, stop=True).then_inc(rank_mm, 1)

            rows(0)
            for c in range(len(CHUNKS)):
                g0, ng = chunk0[c] // GT, CHUNKS[c] // GT
                if c >= 1:
                    ranks(c - 1)
                if c + 1 < len(CHUNKS):
                    rows(c + 1)
                if c >= 2:
                    pe.wait_ge(routed, c - 1)
                for g in range(g0, g0 + ng):
                    z_cols(g, g % 2, g < 2)
                    if g > g0:
                        logits(g - 1, (g - 1) % 2, c)
                logits(g0 + ng - 1, (g0 + ng - 1) % 2, c)
            ranks(len(CHUNKS) - 1)
            pe.wait_ge(etab_ok, len(CHUNKS))
            pe.wait_ge(split, 4 * E + 1)

            def zT(g, i, turn, first=False):
                if not first:
                    pe.wait_ge(zl_ok, g)
                if i % UNIT == 0:
                    pe.wait_ge(slot_in[i // UNIT], turn)
                nc.tensor.transpose(psz, zslot[:, i, 0:C], ident[:, :]).then_inc(zT_mm, 1)

            def w13_at(e, part, c0, n):
                return w13s[:, ds(e * (4 * HF) + (part * 2 * HF + c0), n)]

            def w2_at(e, j, k):
                return w2s[0:k, ds(e * (6 * C) + j * 2 * C, 2 * C)]

            def h13(g, i, e):
                b = i % 2
                cols = ((ps13[b][:, 0:HA], 0, HA), (ps13[b][:, HA:2 * HF], HA, HB))
                for z, part, st, sp_ in ((zTh, 0, True, False), (zTh, 1, False, False), (zTl, 0, False, True)):
                    for o, c0, n in cols:
                        ins = mm(o, z[:, b, :], w13_at(e, part, c0, n), start=st, stop=sp_)
                ins.then_inc(h13_mm, 1)

            def hT(g, i):
                pe.wait_ge(h_ok, g + 1)
                for j in range(3):
                    ins = nc.tensor.transpose(psh[i % 2][:, j * P:(j + 1) * P], hsl[:, i % 2, j * KC:(j + 1) * KC], ident[:, :])
                ins.then_inc(hT_mm, 1)

            def y(g, i, e):
                pe.wait_ge(hTl_ok, g + 1)
                if not (i == 0 and isinstance(g, int) and g == 0):
                    pe.wait_ge(y_ev, g)
                for j, k in enumerate(KJ):
                    for h in (hTh, hTl):
                        ins = mm(psy, h[0:k, i % 2, j * P:(j + 1) * P], w2_at(e, j, k),
                                 start=(j == 0 and h is hTh), stop=(j == 2 and h is hTl))
                ins.then_inc(y_mm, 1)

            def experts(g, n):
                return nc.values_load_multi_w_load_instructions(
                    etab[0:1, ds(g, n)], engines=(mybir.EngineType.PE,), min_val=0, max_val=E - 1,
                    skip_runtime_bounds_check_because="the table is clamped to E - 1 and counts from 0")[1]

            def addresses(e, e2):
                if e is not None:
                    for part in range(2):
                        for c0, n in ((0, HA), (HA, HB)):
                            pe.lower_ap(w13_at(e, part, c0, n))
                if e2 is not None:
                    for j, k in enumerate(KJ):
                        pe.lower_ap(w2_at(e2, j, k))

            zT(0, 0, 16, True)
            ex = experts(0, RING)
            for g in range(RING):
                zT(g + 1, (g + 1) % RING, 16 * ((g + 1) // RING + 1))
                h13(g, g, ex[g])
                if g >= 1:
                    hT(g - 1, g - 1)
                if g >= 2:
                    y(g - 2, g - 2, ex[g - 2])
            with pe.Fori(1, NS // RING - 1) as r:
                ex = experts(r * RING - 4, RING + 4)
                for i in range(RING):
                    g = r * RING + i
                    addresses(ex[i + 4], ex[i + 2])
                    zT(g + 1, (i + 1) % RING, r * 16 + (16 if i < RING - 1 else 32))
                    h13(g, i, ex[i + 4])
                    hT(g - 1, i - 1)
                    y(g - 2, i - 2, ex[i + 2])
            ex = experts(NS - RING - 4, RING + 4)
            for i in range(RING + 2):
                g = NS - RING + i
                if i < RING - 1:
                    zT(g + 1, i + 1, 16 * (NS // RING))
                if i == RING - 1:
                    pe.wait_ge(zl_ok, NS)
                if i < RING:
                    h13(g, i, ex[i + 4])
                if i < RING + 1:
                    hT(g - 1, i - 1)
                y(g - 2, i - 2, ex[i + 2])


def kernel(x, adj, L0_gnn_W1, L0_gnn_b1, L0_gnn_g1, L0_gnn_be1, L0_gnn_W2, L0_gnn_b2, L0_gnn_g2, L0_gnn_be2,
           L0_ffn_router_w, L0_ffn_w1, L0_ffn_w2, L0_ffn_w3):
    import numpy as np
    import concourse.bacc as bacc
    from concourse import mybir
    from concourse.bass_utils import run_bass_kernel_spmd as run

    c = np.ascontiguousarray
    a = lambda v: np.asarray(v)
    cols = lambda v: a(v).reshape(-1, P).T
    w13 = np.concatenate([a(L0_ffn_w1), a(L0_ffn_w3)], axis=1)
    arrays = {
        "x_rows": c(a(x).reshape(TOK, C)),
        "adj_in": c(a(adj)),
        "gnn_w1_t": c(a(L0_gnn_W1).T),
        "gnn_w2_t": c(a(L0_gnn_W2).T),
        "gnn_vectors": c(np.concatenate([cols(L0_gnn_b1), cols(L0_gnn_g1), cols(L0_gnn_be1), cols(L0_gnn_b2),
                                         cols(L0_gnn_g2), cols(L0_gnn_be2)], axis=1)),
        "router_t": c(a(L0_ffn_router_w).T),
        "w13_t": c(w13.transpose(2, 0, 1).reshape(C, E * 2 * HF)),
        "w2_t": c(a(L0_ffn_w2).transpose(0, 2, 1).reshape(E * HF, C)),
    }
    nc = bacc.Bacc("TRN2", target_bir_lowering=False, num_devices=1)
    args = [nc.dram_tensor(k, v.shape, mybir.dt.from_np(v.dtype), kind="ExternalInput").ap() for k, v in arrays.items()]
    out = nc.dram_tensor("out_rows", (TOK, C), mybir.dt.float32, kind="ExternalOutput").ap()
    build(nc, *args, out)
    got = run(nc, [arrays], core_ids=[0])
    return got.results[0]["out_rows"].reshape(B, N, C)
```

```python
import concourse.bass as bass
from concourse import mybir
from contextlib import ExitStack

P = 128
B, N, C = 128, 64, 128
TOK = B * N
T = TOK // P
GT = 4
GR = T // GT
GC = GT * P
XPARTS = ((0, 2), (2, 6), (6, 16))
RG = 8
HID = 256
HALVES = HID // P
E, TOPK, HF = 8, 2, 341
EPS = 1e-5
ACT_TILES = 2
CHUNKS = (16, 32, 16)
RING = 8
UNIT = 2
UNITS = RING // UNIT
SLOTS = tuple(-(-(TOPK * nt + E - 1) // RING) * RING for nt in CHUNKS)
NS = sum(SLOTS)
ROW = C + 2
HA = 342
HB = 2 * HF - HA
PAD = 512 - HA
KC = 114
KJ = (KC, KC, HF - 2 * KC)


def build(nc, x, adj, gw1, gw2, gvec, rw, w13, w2, out):
    f32, f32r, i32 = mybir.dt.float32, mybir.dt.float32r, mybir.dt.int32
    ACT, ALU, AX = mybir.ActivationFunctionType, mybir.AluOpType, mybir.AxisListType.X
    ds = bass.ds
    V, S = nc.vector, nc.scalar
    chunk0 = [sum(CHUNKS[:c]) for c in range(len(CHUNKS))]
    slot0 = [sum(SLOTS[:c]) for c in range(len(CHUNKS))]
    NTX, NSX = max(CHUNKS), max(SLOTS)
    G = [t // GT for t in chunk0] + [GR]
    MID = (G[1] + G[2]) // 2
    PARTS = ((0, G[1]), (G[1], MID), (MID, G[2]), (G[2], GR))

    sent = [nc.dram_tensor(f"sent{c}", [s * P, ROW], f32, kind="Internal").ap() for c, s in enumerate(SLOTS)]
    back = nc.dram_tensor("back", [SLOTS[0] * P, C], f32, kind="Internal").ap()
    home = [None] + [nc.dram_tensor(f"home{c}", [TOPK * CHUNKS[c] * P, C], f32, kind="Internal").ap()
                     for c in range(1, len(CHUNKS))]

    with ExitStack() as ctx:
        def sb(name, shape, dt=f32):
            return ctx.enter_context(nc.sbuf_tensor(name, shape, dt))

        def sem(name):
            return ctx.enter_context(nc.semaphore(name))

        xs = sb("xs", [P, T, C])
        big = sb("big", [P, 2 * TOK + 2 * T])
        hid = [big[:, h * TOK:(h + 1) * TOK] for h in range(HALVES)]
        gout = hid[0]
        zrow = big[:, TOK:TOK + T * ROW].rearrange("p (t r) -> p t r", r=ROW)
        w13s = sb("w13s", [P, E * 2 * 2 * HF], f32r)
        w2s = sb("w2s", [KC, E * 3 * 2 * C], f32r)
        zTh, zTl = sb("zTh", [P, 2, P], f32r), sb("zTl", [P, 2, P], f32r)
        hTh, hTl = sb("hTh", [KC, 2, 3 * P], f32r), sb("hTl", [KC, 2, 3 * P], f32r)

        arena = sb("arena", [P, RG * GT * C + 2 * GC + 2 * HF + 3 * C])
        at = [0]

        def part(n):
            at[0] += n
            return arena[:, at[0] - n:at[0]]

        fring = part(RG * GT * C).rearrange("p (t c) -> p t c", c=C)
        aggT = part(2 * GC).rearrange("p (b n) -> p b n", b=2)
        st13 = part(2 * HF)
        st2 = part(3 * C)
        at[0] = 0
        zslot = part(RING * ROW).rearrange("p (s r) -> p s r", r=ROW)
        lists_at = at[0]
        sil = part(2 * HF).rearrange("p (b n) -> p b n", b=2)
        hsl = part(2 * 3 * KC).rearrange("p (b n) -> p b n", b=2)
        ysl = part(RING * C).rearrange("p (s c) -> p s c", c=C)
        zTr = part(2 * GC).rearrange("p (b n) -> p b n", b=2)
        slot_cmp, so_e = part(E * NSX)[0:1, :], part(NSX)[0:1, :]
        at[0] = lists_at
        tmp = [part(E * NTX) for _ in range(5)]
        pair = [part(TOPK * E * NTX), arena[:, lists_at:lists_at + TOPK * E * NTX]]
        ran = part(E * NTX + 1)

        def home_of(g):
            return big[:, (g - G[1]) * GT * TOPK * C:(g - G[1] + 1) * GT * TOPK * C].rearrange(
                "p (t k c) -> p t k c", k=TOPK, c=C)

        ident, ones = sb("ident", [P, P]), sb("ones", [P, P])
        blk, ahat = sb("blk", [P, P]), sb("ahat", [P, P])
        gw1s, gw2s = sb("gw1s", [P, HID]), sb("gw2s", [P, HALVES, C])
        vec, rws = sb("vec", [P, 9]), sb("rws", [P, E])
        b1, g1, be1 = vec[:, 0:2], vec[:, 2:4], vec[:, 4:6]
        b2, g2, be2 = vec[:, 6:7], vec[:, 7:8], vec[:, 8:9]
        blank = sb("blank", [P, ROW])
        st6 = sb("st6", [P, T, 6])
        hst = sb("hst", [P, HALVES, GR * 6])
        ost = sb("ost", [P, GR * 6])
        mean, rstd, nmr = sb("mean", [P, T]), sb("rstd", [P, T]), sb("nmr", [P, T])
        rv, rs, rt = sb("rv", [P, T]), sb("rs", [P, T]), sb("rt", [P, T])
        mv = sb("mv", [P, HALVES, 2])
        bnsc, bnsh = sb("bnsc", [P, 3]), sb("bnsh", [P, 3])
        deg = sb("deg", [P, 4])
        revi, rev = sb("revi", [P, E], i32), sb("rev", [P, E])
        so = sb("so", [1, NSX])
        gate2 = sb("gate2", [P, T])
        idx = sb("idx", [P, TOPK, T], i32)
        etab = sb("etab", [1, NS], i32)
        soi = etab[:, 0:NSX]
        dest = sb("dest", [P, RING], i32)
        sm = sb("sm", [P, 6, NTX])
        cnt = sb("cnt", [P, 4, E])
        cnti = sb("cnti", [P, 2, E], i32)
        before = sb("before", [P, P])

        ps = ctx.enter_context(nc.psum_tensor("ps", [P, 8, 512], f32))
        psA = [ps[:, b, :] for b in (0, 1)]
        psH = [ps[:, 2 + 2 * b:4 + 2 * b, :] for b in (0, 1)]
        psT = [ps[:, b, :] for b in (2, 3, 1)]
        psZ = [ps[:, b, :] for b in (4, 5)]
        psL = [ps[:, b, :] for b in (6, 7)]
        psR = ps[:, 0, :]
        flat = ps[:, :, :].rearrange("p b n -> p (b n)")
        ps13 = [flat[:, 1024 * b + PAD:1024 * b + PAD + 2 * HF] for b in (0, 1)]
        psz = ps[:, 4, 0:P]
        psh = ps[0:KC, 5, 0:3 * P]
        psy = [ps[:, b, 0:2 * C] for b in (6, 7)]

        x_in = [sem(f"x_in{q}") for q in range(len(XPARTS))]
        adj_in, par_in, par2_in = sem("adj_in"), sem("par_in"), sem("par2_in")
        stage13_in, stage2_in = sem("stage13_in"), sem("stage2_in")
        zeroed, blanked = sem("zeroed"), sem("blanked")
        consts, cleared = sem("consts"), sem("cleared")
        split = sem("split")
        stat_ok = sem("stat_ok")
        dseq = sem("dseq")
        root_in, root_out = sem("root_in"), sem("root_out")
        adj_col, adj_sc, adj_T, adj_ok = sem("adj_col"), sem("adj_sc"), sem("adj_T"), sem("adj_ok")
        nmr_ok, f_act = sem("nmr_ok"), sem("f_act")
        f_ready, agg_mm, agg_ev = sem("f_ready"), sem("agg_mm"), sem("agg_ev")
        hid_mm, hid_ev = sem("hid_mm"), sem("hid_ev")
        bn1_ok, bn2_ok, relu_ok = sem("bn1_ok"), sem("bn2_ok"), sem("relu_ok")
        out_mm, out_ev = sem("out_mm"), sem("out_ev")
        bnout, outT_mm, x2_ok = sem("bnout"), sem("outT_mm"), sem("x2_ok")
        z_dve = sem("z_dve")
        z_ok, zr_mm, zr_ev, logit_mm = sem("z_ok"), sem("zr_mm"), sem("zr_ev"), sem("logit_mm")
        ex_in, ex_out = sem("ex_in"), sem("ex_out")
        v2_ok, sel_ok, rank_mm = sem("v2_ok"), sem("sel_ok"), sem("rank_mm")
        routed, etab_ok = sem("routed"), sem("etab_ok")
        sent_k0, sent_k1 = [sem(f"sent_k0_{h}") for h in range(2)], sem("sent_k1")
        regate = sem("regate")
        slot_in = [sem(f"slot_in{u}") for u in range(UNITS)]
        slot_out = [sem(f"slot_out{u}") for u in range(UNITS)]
        slot_home = [sem(f"slot_home{u}") for u in range(UNITS)]
        zT_mm, zh_ok, zl_ok = sem("zT_mm"), sem("zh_ok"), sem("zl_ok")
        h13_mm, silu_ok, h_ok = sem("h13_mm"), sem("silu_ok"), sem("h_ok")
        hT_mm, hTh_ok, hTl_ok = sem("hT_mm"), sem("hTh_ok"), sem("hTl_ok")
        y_mm, y_lo, y_ev = sem("y_mm"), sem("y_lo"), sem("y_ev")
        got_k0, got_k1 = [sem(f"got_k0_{h}") for h in range(2)], sem("got_k1")
        dest_ok, summed, added = sem("dest_ok"), sem("summed"), sem("added")
        home_in = {g: sem(f"home_in{g}") for g in range(G[1], GR)}
        home_end = sem("home_end")
        stored = sem("stored")

        block = ctx.enter_context(nc.Block())

        @block.sync
        def _(sp):
            xv = x.rearrange("(t p) c -> p t c", p=P)

            def load_x(q):
                a, b = XPARTS[q][0] * GT, XPARTS[q][1] * GT
                sp.dma_start(xs[:, a:b, :], xv[:, a:b, :]).then_inc(x_in[q], 16)

            sp.dma_start(blk[0:N, 0:N], adj).then_inc(adj_in, 16)
            sp.dma_start(blk[N:P, N:P], adj).then_inc(adj_in, 16)
            load_x(0)
            sp.dma_start(gw1s[:, :], gw1).then_inc(par_in, 16)
            sp.dma_start(vec[:, :], gvec).then_inc(par_in, 16)
            for q in range(1, len(XPARTS)):
                load_x(q)
            sp.dma_start(gw2s[:, :, :], gw2.rearrange("(h p) o -> p h o", p=P)).then_inc(par2_in, 16)
            sp.dma_start(rws[:, :], rw).then_inc(par2_in, 16)
            with sp.Fori(0, E) as e:
                sp.wait_ge(split, e * 4 + 1)
                sp.dma_start(st13, w13[:, ds(e * (2 * HF), 2 * HF)]).then_inc(stage13_in, 16)
                sp.dma_start(st2[0:KC, :].rearrange("p (j c) -> p j c", j=3)[:, 0:2, :],
                             w2[ds(e * HF, 2 * KC), :].rearrange("(j p) c -> p j c", p=KC)).then_inc(stage2_in, 16)
                sp.dma_start(st2[0:KJ[2], 2 * C:3 * C], w2[ds(e * HF + 2 * KC, KJ[2]), :]).then_inc(stage2_in, 16)

            def load(c, u, row):
                sp.dma_start(zslot[:, UNIT * u:UNIT * u + UNIT, :],
                             sent[c][ds(row, UNIT * P), :].rearrange("(s p) r -> p s r", p=P)).then_inc(slot_in[u], 16)

            def store_back(u, row, done):
                sp.wait_ge(y_ev, done)
                sp.dma_start(back[ds(row, UNIT * P), :].rearrange("(s p) c -> p s c", p=P),
                             ysl[:, UNIT * u:UNIT * u + UNIT, :]).then_inc(slot_out[u], 16)

            def freed(turn, u):
                sp.wait_ge(y_ev, turn * RING + (u * UNIT + UNIT - RING))

            def rows_sent(c):
                sp.wait_ge(sent_k1, 16 * (chunk0[c] + CHUNKS[c]))

            RP = RING * P
            rows_sent(0)
            for u in range(UNITS):
                load(0, u, u * UNIT * P)
            with sp.Fori(1, SLOTS[0] // RING) as r:
                for u in range(UNITS):
                    store_back(u, r * RP + (u * UNIT - RING) * P, r * RING + (u * UNIT + UNIT - RING))
                    load(0, u, r * RP + u * UNIT * P)
            rows_sent(1)
            for u in range(UNITS):
                store_back(u, (SLOTS[0] - RING + u * UNIT) * P, SLOTS[0] - RING + u * UNIT + UNIT)
                load(1, u, u * UNIT * P)
            with sp.Fori(1, SLOTS[1] // RING) as r:
                for u in range(UNITS):
                    freed(SLOTS[0] // RING + r, u)
                    load(1, u, r * RP + u * UNIT * P)
            rows_sent(2)
            ov = out.rearrange("(t p) c -> p t c", p=P)

            def store(g, groups=1):
                sp.dma_start(ov[:, g * GT:(g + groups) * GT, :], xs[:, g * GT:(g + groups) * GT, :]).then_inc(stored, 16)

            def load_home(g, c):
                rows = home[c][(g - G[c]) * GT * TOPK * P:(g + 1 - G[c]) * GT * TOPK * P, :]
                sp.dma_start(home_of(g), rows.rearrange("(t p k) c -> p t k c", p=P, k=TOPK)).then_inc(home_in[g], 16)

            for r in range(SLOTS[2] // RING):
                for u in range(UNITS if r == 1 else 0):
                    sp.wait_ge(slot_home[u], 32 * (SLOTS[1] // RING))
                for u in range(UNITS):
                    freed((SLOTS[0] + SLOTS[1]) // RING + r, u)
                    load(2, u, r * RP + u * UNIT * P)
                    n = r * UNITS + u - UNITS
                    if 0 <= n < G[2] - G[1]:
                        load_home(G[1] + n, 1)
            sp.wait_ge(got_k1, 16 * CHUNKS[0])
            store(0, G[1])
            for g in range(G[1], G[2]):
                sp.wait_ge(added, g - G[1] + 1)
                store(g)
            for u in range(UNITS):
                sp.wait_ge(slot_home[u], 32 * ((NS - SLOTS[0]) // RING))
            for g in range(G[2], GR - 1):
                load_home(g, 2)
            for t, there in ((0, home_in[GR - 1]), (GT // 2, home_end)):
                row = ((GR - 1 - G[2]) * GT + t) * TOPK * P
                rows = home[2][row:row + GT // 2 * TOPK * P, :]
                sp.dma_start(home_of(GR - 1)[:, t:t + GT // 2, :, :],
                             rows.rearrange("(t p k) c -> p t k c", p=P, k=TOPK)).then_inc(there, 16)
            for g in range(G[2], GR - 1):
                sp.wait_ge(added, g - G[1] + 1)
                store(g)
            for h in range(2):
                sp.wait_ge(added, GR - 1 - G[1] + h + 1)
                t = (GR - 1) * GT + h * GT // 2
                sp.dma_start(ov[:, t:t + GT // 2, :], xs[:, t:t + GT // 2, :]).then_inc(stored, 16)
            sp.wait_ge(stored, 16 * (2 + GR - G[1]))

        @block.gpsimd
        def _(gp):
            gp.memset(blk[0:N, N:P], 0.0).then_inc(cleared, 1)
            gp.memset(blk[N:P, 0:N], 0.0).then_inc(cleared, 1)
            gp.wait_ge(cleared, 2)
            gp.memset(st2, 0.0).then_inc(split, 1)
            gp.memset(blank[:, :], 0.0).then_inc(consts, 1)
            gp.memset(ident[:, :], 0.0).then_inc(consts, 1)
            gp.memset(ones[:, :], 1.0).then_inc(consts, 1)
            gp.iota(revi[:, :], [[-1, E]], base=E, channel_multiplier=0).then_inc(consts, 1)
            gp.iota(soi, [[1, NSX]], base=0, channel_multiplier=0).then_inc(consts, 1)
            gp.wait_ge(consts, 5)
            gp.affine_select(out=ident[:, :], in_=ident[:, :], compare_op=ALU.not_equal, fill=1.0,
                             base=0, pattern=[[-1, P]], channel_multiplier=1).then_inc(consts, 1)
            gp.affine_select(out=before[:, :], in_=blank[:, 0:P], compare_op=ALU.is_gt, fill=-1.0,
                             base=0, pattern=[[1, P]], channel_multiplier=-1).then_inc(consts, 1)
            gp.tensor_copy(rev[:, :], revi[:, :]).then_inc(consts, 1)
            gp.tensor_copy(so[:, :], soi).then_inc(consts, 1)
            gp.iota(blank[:, C + 1:ROW].bitcast(i32), [[0, 1]], base=TOPK * TOK, channel_multiplier=0).then_inc(blanked, 1)
            gp.wait_ge(blanked, 1)
            gp.wait_ge(x_in[-1], 16)
            for c, s in enumerate(SLOTS):
                gp.dma_start(sent[c].rearrange("(p s) r -> p s r", p=P),
                             blank[:, :].unsqueeze(1).broadcast_to([P, s, ROW])).then_inc(zeroed, 16)
            with gp.Fori(0, E) as e:
                gp.wait_ge(stage13_in, e * 16 + 16)
                hi, lo = ds(e * (4 * HF), 2 * HF), ds(e * (4 * HF) + 2 * HF, 2 * HF)
                gp.tensor_copy(w13s[:, hi], st13).then_inc(split, 1)
                gp.wait_ge(split, e * 4 + 2)
                gp.tensor_tensor(w13s[:, lo], st13, w13s[:, hi].bitcast(f32), ALU.subtract).then_inc(split, 1)
                gp.wait_ge(stage2_in, e * 32 + 32)
                parts = w2s[:, ds(e * (6 * C), 6 * C)].rearrange("p (j b c) -> p j b c", j=3, b=2)
                raw = st2[0:KC, :].rearrange("p (j c) -> p j c", j=3)
                gp.tensor_copy(parts[:, :, 0, :], raw).then_inc(split, 1)
                gp.wait_ge(split, e * 4 + 4)
                gp.tensor_tensor(parts[:, :, 1, :], raw, parts[:, :, 0, :].bitcast(f32), ALU.subtract).then_inc(split, 1)
            gp.wait_ge(zeroed, 16 * len(CHUNKS))
            halves = [((t0, t0 + nt // 2), (t0 + nt // 2, t0 + nt)) for t0, nt in zip(chunk0, CHUNKS)]
            done0 = [0, 0]
            for c, nt in enumerate(CHUNKS):
                gp.wait_ge(routed, c + 1)
                for k in range(TOPK):
                    for h, (a, b) in enumerate(halves[c]):
                        if k:
                            gp.wait_ge(sent_k0[h], 16 * done0[h])
                            gp.tensor_copy(zrow[:, a:b, C], gate2[:, a:b]).then_inc(regate, 1)
                        else:
                            done0[h] += b - a
                        gp.iota(zrow[:, a:b, C + 1].bitcast(i32), [[TOPK * P, b - a]],
                                base=(a - chunk0[c]) * TOPK * P + k, channel_multiplier=TOPK).then_inc(dest_ok, 1)
                        if k:
                            gp.wait_ge(regate, 2 * c + h + 1)
                        gp.wait_ge(dest_ok, 4 * c + 2 * k + h + 1)
                        for t in range(a, b):
                            gp.indirect_dma_start(sent[c], bass.IndirectOffsetOnAxis(idx[:, k, t:t + 1], 0),
                                                  zrow[:, t, :], None).then_inc(sent_k1 if k else sent_k0[h], 16)
            gathers = [(k, h, t) for k in range(TOPK) for h, (a, b) in enumerate(halves[0]) for t in range(a, b)]

            def scatter(n, c):
                i = n % RING
                gp.wait_ge(y_ev, SLOTS[0] + n + 1)
                gp.indirect_dma_start(home[c], bass.IndirectOffsetOnAxis(dest[:, i:i + 1], 0),
                                      ysl[:, i, :], None, bounds_check=TOPK * CHUNKS[c] * P - 1,
                                      oob_is_err=False).then_inc(slot_home[i // UNIT], 16)

            for n in range(SLOTS[1]):
                if n == RING:
                    for u in range(UNITS):
                        gp.wait_ge(slot_out[u], 16 * (SLOTS[0] // RING))
                scatter(n, 1)
                done, due = ((m - RING) * len(gathers) // (SLOTS[1] - RING) for m in (n, n + 1))
                for k, h, t in gathers[max(done, 0):max(due, 0)]:
                    if k and t == halves[0][h][0]:
                        gp.wait_ge(got_k0[h], 16 * (halves[0][h][1] - halves[0][h][0]))
                    gp.indirect_dma_start(xs[:, t, :], None, back, bass.IndirectOffsetOnAxis(idx[:, k, t:t + 1], 0),
                                          compute_op=ALU.add).then_inc(got_k1 if k else got_k0[h], 16)

            for n in range(SLOTS[2]):
                scatter(SLOTS[1] + n, 2)
                if n >= RING and n - RING < 2 * (G[2] - G[1]):
                    g, step = G[1] + (n - RING) // 2, (n - RING) % 2
                    y = home_of(g)
                    if step == 0:
                        gp.wait_ge(home_in[g], 16)
                        gp.tensor_tensor(y[:, :, 0, :], y[:, :, 0, :], y[:, :, 1, :], ALU.add).then_inc(summed, 1)
                    else:
                        gp.wait_ge(summed, g - G[1] + 1)
                        a = xs[:, g * GT:(g + 1) * GT, :]
                        gp.tensor_tensor(a, a, y[:, :, 0, :], ALU.add).then_inc(added, 1)

        @block.scalar
        def _(act):
            roots = [0]

            def root(cols):
                roots[0] += 1
                act.wait_ge(root_in, roots[0])
                S.activation(rs[:, cols], rv[:, cols], ACT.Sqrt).then_inc(root_out, 1)

            root(slice(0, 1))

            def ln_tile(g):
                if g >= RG:
                    act.wait_ge(agg_mm, g - RG + 1)
                for t in range((g + 1) * GT - ACT_TILES, (g + 1) * GT):
                    ins = S.activation(fring[:, t % (RG * GT), :], xs[:, t, :], ACT.Identity,
                                       bias=nmr[:, t:t + 1], scale=rstd[:, t:t + 1])
                ins.then_inc(f_act, 1)

            def agg_out(g, b, first=False):
                act.wait_ge(agg_mm, g + 1)
                if not first:
                    act.wait_ge(hid_mm, g * 2 - 2)
                S.activation(aggT[:, b, :], psA[b], ACT.Copy).then_inc(agg_ev, 1)

            def hid_out(g, b):
                for h in range(HALVES):
                    act.wait_ge(hid_mm, g * 2 + (h + 1))
                    S.activation(hid[h][:, ds(g * GC, GC)], psH[b][:, h, :], ACT.Identity,
                                 bias=b1[:, h:h + 1]).then_inc(hid_ev, 1)

            def ln_part(q, groups):
                a, b = XPARTS[q]
                root(slice(a * GT, b * GT))
                act.wait_ge(nmr_ok, q + 1)
                for g in range(a, a + groups):
                    ln_tile(g)

            g1, g2 = XPARTS[1]
            ln_part(0, g1)
            agg_out(0, 0, True)
            ln_part(1, g2 - g1)
            act.wait_ge(par_in, 32)
            for g in range(GR):
                for q, (a, b) in enumerate(XPARTS):
                    if q >= 2 and g == a - 2:
                        ln_part(q, 2)
                if g + 1 < GR:
                    agg_out(g + 1, (g + 1) % 2, g == 0)
                hid_out(g, g % 2)
                if g + 3 < GR and g + 3 not in [n for a, b in XPARTS for n in (a, a + 1)] and g + 3 >= g2:
                    ln_tile(g + 3)
            root(slice(0, 2))
            act.wait_ge(bn1_ok, 1)
            with act.Fori(0, GR) as g:
                for h in range(HALVES):
                    S.activation(hid[h][:, ds(g * GC, GC)], hid[h][:, ds(g * GC, GC)], ACT.Relu,
                                 bias=bnsh[:, h:h + 1], scale=bnsc[:, h:h + 1]).then_inc(relu_ok, 1)
            root(slice(0, 1))
            act.wait_ge(bn2_ok, 1)

            def bn_apply(c):
                for g in range(chunk0[c] // GT, (chunk0[c] + CHUNKS[c]) // GT):
                    a = gout[:, g * GC:(g + 1) * GC]
                    S.activation(a, a, ACT.Identity, bias=bnsh[:, 2:3], scale=bnsc[:, 2:3]).then_inc(bnout, 1)

            def zr_out(g):
                act.wait_ge(zr_mm, g + 1)
                if g >= 2:
                    act.wait_ge(logit_mm, g - 1)
                S.activation(zTr[:, g % 2, :], psZ[g % 2], ACT.Copy).then_inc(zr_ev, 1)

            def exps(c):
                act.wait_ge(ex_in, c + 1)
                S.activation(tmp[1][:, 0:E * CHUNKS[c]], tmp[0][:, 0:E * CHUNKS[c]], ACT.Exp).then_inc(ex_out, 1)
                act.wait_ge(v2_ok, c + 1)
                S.activation(sm[:, 3, 0:CHUNKS[c]], sm[:, 2, 0:CHUNKS[c]], ACT.Exp).then_inc(ex_out, 1)

            def scales(p):
                root(slice(PARTS[p][0] * GT, PARTS[p][1] * GT))

            def pair_rows(p, exps_of=None):
                g0, g1 = PARTS[p]
                act.wait_ge(nmr_ok, len(XPARTS) + p + 1)
                for g in range(g0, g1):
                    for t in range(g * GT, (g + 1) * GT - 1):
                        ins = S.activation(zrow[:, t, 0:C], xs[:, t, :], ACT.Identity,
                                           bias=nmr[:, t:t + 1], scale=rstd[:, t:t + 1])
                    ins.then_inc(z_ok, 1)
                    if g > g0:
                        zr_out(g - 1)
                    if exps_of is not None and g == g0 + 1:
                        exps(exps_of)
                zr_out(g1 - 1)

            bn_apply(0)
            bn_apply(1)
            scales(0)
            pair_rows(0)
            scales(1)
            bn_apply(2)
            pair_rows(1, exps_of=0)
            scales(2)
            pair_rows(2)
            scales(3)
            pair_rows(3, exps_of=1)
            exps(2)

            def z_hi(g, i):
                act.wait_ge(zT_mm, g + 1)
                S.activation(zTh[:, i % 2, :], psz, ACT.Copy).then_inc(zh_ok, 1)

            def silu(g, i):
                act.wait_ge(h13_mm, g + 1)
                S.activation(sil[:, i % 2, :], ps13[i % 2][:, 0:HF], ACT.Silu).then_inc(silu_ok, 1)

            def hT_hi(g, i):
                act.wait_ge(hT_mm, g + 1)
                S.activation(hTh[:, i % 2, :], psh, ACT.Copy).then_inc(hTh_ok, 1)

            R0 = SLOTS[0] // RING

            def y_low(g, i, turn, by_pool=False):
                act.wait_ge(y_mm, g + 1)
                if i % UNIT == 0 and by_pool:
                    act.wait_ge(slot_home[i // UNIT], turn * 32 - R0 * 32)
                elif i % UNIT == 0 and not (isinstance(turn, int) and turn == 0):
                    act.wait_ge(slot_out[i // UNIT], turn * 16)
                S.activation(ysl[:, i, :], psy[i % 2][:, C:2 * C], ACT.Copy, scale=zslot[:, i, C:C + 1]).then_inc(y_lo, 1)

            def turn(r, old=False, new=False):
                for i in range(RING):
                    g = r * RING + i
                    z_hi(g + 1, i + 1)
                    silu(g, i)
                    if i or not (isinstance(r, int) and r == 0):
                        hT_hi(g - 1, i - 1)
                    if i >= 2:
                        y_low(g - 2, i - 2, r, new)
                    elif not (isinstance(r, int) and r == 0):
                        y_low(g - 2, i + RING - 2, r - 1, old)

            z_hi(0, 0)
            turn(0)
            turn(1)
            with act.Fori(2, R0 + 1) as r:
                turn(r)
            turn(R0 + 1, old=False, new=True)
            with act.Fori(R0 + 2, NS // RING - 1) as r:
                turn(r, old=True, new=True)
            for i in range(RING + 2):
                g = NS - RING + i
                if i < RING - 1:
                    z_hi(g + 1, i + 1)
                if i < RING:
                    silu(g, i)
                if i < RING + 1:
                    hT_hi(g - 1, i - 1)
                y_low(g - 2, (i - 2) % RING, (g - 2) // RING, True)

        @block.vector
        def _(dve):
            seq, roots, seen = [0], [0], [0]

            def link(ins):
                seq[0] += 1
                ins.then_inc(dseq, 1)
                dve.wait_ge(dseq, seq[0])

            def begin(ins):
                seq[0] += 1
                return ins.then_inc(dseq, 1)

            def all_done():
                dve.wait_ge(dseq, seq[0])

            def stats(groups):
                seen[0] += groups
                dve.wait_ge(stat_ok, seen[0])

            def rsqrt(dst, cols):
                roots[0] += 1
                a = rv[:, cols]
                dve.wait_ge(root_out, roots[0])
                link(V.reciprocal(dst, rs[:, cols]))
                link(V.tensor_tensor(rt[:, cols], dst, dst, ALU.mult))
                link(V.scalar_tensor_tensor(rt[:, cols], rt[:, cols], -0.5, a, ALU.mult, ALU.mult))
                link(V.scalar_tensor_tensor(dst, rt[:, cols], 1.5, dst, ALU.add, ALU.mult))

            dve.wait_ge(consts, 9)
            dve.wait_ge(cleared, 2)
            dve.wait_ge(adj_in, 32)
            link(V.tensor_tensor(blk[:, :], blk[:, :], ident[:, :], ALU.add))
            V.tensor_reduce(deg[:, 0:1], blk[:, :], AX, ALU.add).then_inc(adj_sc, 1)
            link(V.tensor_tensor(ahat[:, :], blk[:, :], ident[:, :], ALU.mult))
            link(V.tensor_reduce(deg[:, 1:2], ahat[:, :], AX, ALU.add))
            link(V.tensor_tensor(deg[:, 2:3], deg[:, 0:1], deg[:, 1:2], ALU.subtract))
            dve.wait_ge(adj_col, 1)
            V.tensor_tensor(rv[:, 0:1], psA[0][:, 0:1], deg[:, 2:3], ALU.add).then_inc(root_in, 1)
            rsqrt(deg[:, 3:4], slice(0, 1))
            V.tensor_scalar(blk[:, :], blk[:, :], deg[:, 3:4], None, ALU.mult).then_inc(adj_sc, 1)
            dve.wait_ge(adj_T, 1)
            V.tensor_scalar(ahat[:, :], psA[1][:, 0:P], deg[:, 3:4], None, ALU.mult).then_inc(adj_ok, 1)

            def ln_stats(t0, n):
                cols = slice(t0, t0 + n)
                s = st6[:, cols, :]
                begin(V.tensor_tensor(rs[:, cols], s[:, :, 1], s[:, :, 4], ALU.subtract))
                begin(V.tensor_tensor(mean[:, cols], s[:, :, 1], s[:, :, 4], ALU.add))
                link(V.tensor_tensor(rv[:, cols], s[:, :, 2], s[:, :, 5], ALU.add))
                begin(V.scalar_tensor_tensor(rt[:, cols], rs[:, cols], 0.25, rs[:, cols], ALU.mult, ALU.mult))
                begin(V.tensor_scalar(rv[:, cols], rv[:, cols], 1.0 / C, EPS, ALU.mult, ALU.add))
                link(V.tensor_scalar(mean[:, cols], mean[:, cols], 0.5, None, ALU.mult))
                V.tensor_tensor(rv[:, cols], rt[:, cols], rv[:, cols], ALU.add).then_inc(root_in, 1)

            def ln_scales(t0, n):
                cols = slice(t0, t0 + n)
                ln_stats(t0, n)
                rsqrt(rstd[:, cols], cols)
                V.scalar_tensor_tensor(nmr[:, cols], mean[:, cols], -1.0, rstd[:, cols], ALU.mult, ALU.mult).then_inc(nmr_ok, 1)

            def x_stats(q):
                dve.wait_ge(x_in[q], 16)
                for t in range(XPARTS[q][0] * GT, XPARTS[q][1] * GT):
                    ins = V.bn_stats(st6[:, t, :], xs[:, t, :])
                ins.then_inc(stat_ok, 1)

            def ln_group(g):
                if g >= RG:
                    dve.wait_ge(agg_mm, g - RG + 1)
                for t in range(g * GT, (g + 1) * GT - ACT_TILES):
                    ins = V.tensor_scalar(fring[:, t % (RG * GT), :], xs[:, t, :],
                                          mean[:, t:t + 1], rstd[:, t:t + 1], ALU.subtract, ALU.mult)
                ins.then_inc(f_ready, 1)

            def hid_stats(g):
                for h in range(HALVES):
                    dve.wait_ge(hid_ev, g * 2 + h + 1)
                    ins = V.bn_stats(hst[:, h, g * 6:(g + 1) * 6], hid[h][:, g * GC:(g + 1) * GC])
                ins.then_inc(stat_ok, 1)

            for q, (a, b) in enumerate(XPARTS):
                x_stats(q)
                stats(1)
                ln_scales(a * GT, (b - a) * GT)
                for g in range(a, b):
                    ln_group(g)
                    if q >= 2:
                        hid_stats(g - XPARTS[2][0])
            for g in range(GR - XPARTS[2][0], GR):
                hid_stats(g)
            stats(GR)

            def bn_finish(n, gamma, beta, at, done):
                V.tensor_scalar(rv[:, 0:n], mv[:, 0:n, 1], EPS, None, ALU.add).then_inc(root_in, 1)
                rsqrt(rstd[:, 0:n], slice(0, n))
                link(V.tensor_tensor(bnsc[:, at:at + n], rstd[:, 0:n], gamma, ALU.mult))
                link(V.tensor_tensor(rt[:, 0:n], mv[:, 0:n, 0], bnsc[:, at:at + n], ALU.mult))
                V.tensor_tensor(bnsh[:, at:at + n], beta, rt[:, 0:n], ALU.subtract).then_inc(done, 1)

            for h in range(HALVES):
                link(V.bn_aggr(mv[:, h, :], hst[:, h, :]))
            bn_finish(2, g1, be1, 0, bn1_ok)

            def gout_out(g, b):
                dve.wait_ge(out_mm, g + 1)
                a = gout[:, ds(g * GC, GC)]
                V.tensor_scalar(a, psA[b], b2, None, ALU.add).then_inc(out_ev, 1)
                dve.wait_ge(out_ev, g + 1)
                V.bn_stats(ost[:, ds(g * 6, 6)], a).then_inc(stat_ok, 1)

            with dve.Fori(0, GR // 2) as j:
                gout_out(j * 2, 0)
                gout_out(j * 2 + 1, 1)
            stats(GR)
            link(V.bn_aggr(mv[:, 0, :], ost[:, :]))
            bn_finish(1, g2, be2, 2, bn2_ok)

            def residuals(p):
                g0, g1 = PARTS[p]
                for g in range(g0, g1):
                    dve.wait_ge(outT_mm, g + 1)
                    a = xs[:, g * GT:(g + 1) * GT, :].rearrange("p t c -> p (t c)")
                    V.tensor_tensor(a, psT[g % 3], a, ALU.add).then_inc(x2_ok, 1)
                    if g > g0:
                        row_stats(g - 1)
                row_stats(g1 - 1).then_inc(stat_ok, 1)
                stats(1)

            def row_stats(g):
                dve.wait_ge(x2_ok, g + 1)
                for t in range(g * GT, (g + 1) * GT):
                    ins = V.bn_stats(st6[:, t, :], xs[:, t, :])
                return ins

            def route(c):
                t0, nt, ns = chunk0[c], CHUNKS[c], SLOTS[c]
                n = E * nt
                et = lambda a: a.rearrange("p (e t) -> p e t", t=nt)
                te = lambda a: a.rearrange("p (e t) -> p t e", t=nt)
                over_e = lambda a: a.unsqueeze(1).broadcast_to([P, E, nt])
                over_t = lambda a: a.unsqueeze(2).broadcast_to([P, E, nt])
                mx, k1, v2, e2, den, s = (sm[:, i, 0:nt] for i in range(6))
                d, ex, key, both, pf = (a[:, 0:n] for a in tmp)
                m12, places = (a[:, 0:2 * n].rearrange("p (k n) -> p k n", k=2) for a in pair)
                m1, m2 = m12[:, 0, :], m12[:, 1, :]
                dve.wait_ge(logit_mm, (t0 + nt) // GT)
                lg = psL[c % 2][:, 0:n].rearrange("p (t e) -> p t e", e=E)
                link(V.tensor_reduce(mx, lg, AX, ALU.max))
                V.tensor_tensor(et(d), lg.rearrange("p t e -> p e t"), over_e(mx), ALU.subtract).then_inc(ex_in, 1)
                dve.wait_ge(ex_in, c + 1)
                link(V.scalar_tensor_tensor(et(key), et(d), 0.0, over_t(rev[:, :]), ALU.is_equal, ALU.mult))
                link(V.tensor_reduce(k1, te(key), AX, ALU.max))
                link(V.tensor_tensor(et(m1), over_t(rev[:, :]), over_e(k1), ALU.is_equal))
                link(V.scalar_tensor_tensor(pf, m1, -1e30, d, ALU.mult, ALU.add))
                V.tensor_reduce(v2, te(pf), AX, ALU.max).then_inc(v2_ok, 1)
                dve.wait_ge(v2_ok, c + 1)
                link(V.tensor_tensor(et(key), et(pf), over_e(v2), ALU.is_equal))
                link(V.tensor_tensor(et(key), et(key), over_t(rev[:, :]), ALU.mult))
                link(V.tensor_reduce(k1, te(key), AX, ALU.max))
                link(V.tensor_tensor(et(m2), over_t(rev[:, :]), over_e(k1), ALU.is_equal))
                V.tensor_tensor(both, m1, m2, ALU.add).then_inc(sel_ok, 1)
                rank, tot = psR[:, 0:n], psR[:, n:2 * n]
                cn, cum, off = (cnt[:, i, :] for i in range(3))
                ends = ran[:, 1:n + 1].rearrange("p (e t) -> p e t", t=nt)[:, :, nt - 1]
                starts = ran[:, 0:n].rearrange("p (e t) -> p e t", t=nt)[:, :, 0]
                cmp = slot_cmp[:, 0:E * ns].rearrange("p (s e) -> p s e", e=E)
                gate1 = zrow[:, t0:t0 + nt, C]
                dve.wait_ge(ex_out, 2 * c + 2)
                begin(V.tensor_reduce(s, te(ex), AX, ALU.add))
                dve.wait_ge(rank_mm, c + 1)
                link(V.tensor_tensor_scan(ran[:, 1:n + 1], ones[:, 0:1].broadcast_to([P, n]), tot, 0.0, ALU.mult, ALU.add))
                begin(V.scalar_tensor_tensor(den, s, 1e-9, e2, ALU.mult, ALU.add))
                link(V.tensor_tensor(cn, ends, starts, ALU.subtract))
                begin(V.tensor_scalar(den, den, 1.0, None, ALU.add))
                link(V.tensor_scalar(cnti[:, 0, :], cn, float(P - 1), None, ALU.add))
                begin(V.reciprocal(gate1, den))
                link(V.tensor_scalar(cnti[:, 1, :], cnti[:, 0, :], P.bit_length() - 1, None, ALU.arith_shift_right))
                begin(V.tensor_tensor(gate2[:, t0:t0 + nt], e2, gate1, ALU.mult))
                link(V.tensor_tensor_scan(cum, ones[:, 0:E], cnti[:, 1, :], 0.0, ALU.mult, ALU.add))
                begin(V.tensor_tensor(pf, rank, ran[:, 1:n + 1], ALU.add))
                link(V.tensor_tensor(off, cum, cnti[:, 1, :], ALU.subtract))
                begin(V.tensor_tensor(cmp, so[0:1, 0:ns].unsqueeze(2).broadcast_to([1, ns, E]),
                                      cum[0:1, :].unsqueeze(1).broadcast_to([1, ns, E]), ALU.is_ge))
                link(V.scalar_tensor_tensor(off, off, float(P), starts, ALU.mult, ALU.subtract))
                begin(V.tensor_reduce(so_e[:, 0:ns], cmp, AX, ALU.add))
                link(V.tensor_tensor(et(pf), et(pf), over_t(off), ALU.add))
                with nc.allow_low_precision(reason="places are whole numbers below 2**24"):
                    V.tensor_scalar(etab[0:1, slot0[c]:slot0[c] + ns], so_e[:, 0:ns], float(E - 1), None,
                                    ALU.min).then_inc(etab_ok, 1)
                    link(V.tensor_tensor(places.rearrange("p k (e t) -> p k e t", t=nt),
                                         m12.rearrange("p k (e t) -> p k e t", t=nt),
                                         et(pf).unsqueeze(1).broadcast_to([P, TOPK, E, nt]), ALU.mult))
                    V.tensor_reduce(idx[:, :, t0:t0 + nt], places.rearrange("p k (e t) -> p k t e", t=nt),
                                    AX, ALU.add).then_inc(routed, 1)

            link(V.memset(ran[:, 0:1], 0.0))

            def pair_rows(p):
                g0, g1 = PARTS[p]
                residuals(p)
                ln_scales(g0 * GT, (g1 - g0) * GT)
                for t in range(g0 * GT + GT - 1, g1 * GT, GT):
                    V.tensor_scalar(zrow[:, t, 0:C], xs[:, t, :], mean[:, t:t + 1], rstd[:, t:t + 1],
                                    ALU.subtract, ALU.mult).then_inc(z_dve, 1)

            pair_rows(0)
            pair_rows(1)
            route(0)
            pair_rows(2)
            pair_rows(3)
            route(1)
            route(2)
            dve.wait_ge(routed, len(CHUNKS))
            link(V.memset(hsl[:, :, HF:3 * KC], 0.0))

            def z_lo(g, i):
                dve.wait_ge(zh_ok, g + 1)
                V.tensor_tensor(zTl[:, i % 2, :], psz, zTh[:, i % 2, :].bitcast(f32), ALU.subtract).then_inc(zl_ok, 1)

            def gated(g, i):
                dve.wait_ge(silu_ok, g + 1)
                V.tensor_tensor(hsl[:, i % 2, 0:HF], ps13[i % 2][:, HF:2 * HF], sil[:, i % 2, :], ALU.mult).then_inc(h_ok, 1)

            def hT_lo(g, i):
                dve.wait_ge(hTh_ok, g + 1)
                V.tensor_tensor(hTl[:, i % 2, :], psh, hTh[:, i % 2, :].bitcast(f32), ALU.subtract).then_inc(hTl_ok, 1)

            def y_out(g, i):
                dve.wait_ge(y_lo, g + 1)
                V.tensor_copy(dest[:, i:i + 1], zslot[:, i, C + 1:ROW].bitcast(i32))
                V.scalar_tensor_tensor(ysl[:, i, :], psy[i % 2][:, 0:C], zslot[:, i, C:C + 1], ysl[:, i, :],
                                       ALU.mult, ALU.add).then_inc(y_ev, 1)

            z_lo(0, 0)
            for g in range(RING):
                z_lo(g + 1, g + 1)
                gated(g, g)
                if g >= 1:
                    hT_lo(g - 1, g - 1)
                if g >= 2:
                    y_out(g - 2, g - 2)
            with dve.Fori(1, NS // RING - 1) as r:
                for i in range(RING):
                    g = r * RING + i
                    z_lo(g + 1, i + 1)
                    gated(g, i)
                    hT_lo(g - 1, i - 1)
                    y_out(g - 2, (i - 2) % RING)
            for i in range(RING + 2):
                g = NS - RING + i
                if i < RING - 1:
                    z_lo(g + 1, i + 1)
                if i < RING:
                    gated(g, i)
                if i < RING + 1:
                    hT_lo(g - 1, i - 1)
                y_out(g - 2, (i - 2) % RING)

            def add_home(y, a):
                link(V.tensor_tensor(y[:, :, 0, :], y[:, :, 0, :], y[:, :, 1, :], ALU.add))
                V.tensor_tensor(a, a, y[:, :, 0, :], ALU.add).then_inc(added, 1)

            dve.wait_ge(added, G[2] - G[1])
            for g in range(G[2], GR - 1):
                dve.wait_ge(home_in[g], 16)
                add_home(home_of(g), xs[:, g * GT:(g + 1) * GT, :])
            for t, there in ((0, home_in[GR - 1]), (GT // 2, home_end)):
                dve.wait_ge(there, 16)
                last = (GR - 1) * GT + t
                add_home(home_of(GR - 1)[:, t:t + GT // 2, :, :], xs[:, last:last + GT // 2, :])

        @block.tensor
        def _(pe):
            mm = nc.tensor.matmul
            pe.wait_ge(adj_sc, 1)
            mm(psA[0][:, 0:1], blk[:, :], ones[:, 0:1], start=True, stop=True).then_inc(adj_col, 1)
            pe.wait_ge(adj_sc, 2)
            nc.tensor.transpose(psA[1][:, 0:P], blk[:, :], ident[:, :]).then_inc(adj_T, 1)
            pe.wait_ge(adj_ok, 1)
            pe.wait_ge(par_in, 32)

            def agg(g, b, ring, first=False):
                pe.wait_ge(f_ready, g + 1)
                pe.wait_ge(f_act, g + 1)
                if not first:
                    pe.wait_ge(agg_ev, g - 1)
                for u in range(GT):
                    ins = mm(psA[b][:, u * P:(u + 1) * P], fring[:, ring + u, :], ahat[:, :], start=True, stop=True)
                ins.then_inc(agg_mm, 1)

            def hidden(g, b, first=False):
                pe.wait_ge(agg_ev, g + 1)
                if not first:
                    pe.wait_ge(hid_ev, g * 2 - 2)
                for h in range(HALVES):
                    mm(psH[b][:, h, :], gw1s[:, h * P:(h + 1) * P], aggT[:, b, :], start=True, stop=True).then_inc(hid_mm, 1)

            agg(0, 0, 0, True)
            for g in range(GR):
                if g + 1 < GR:
                    agg(g + 1, (g + 1) % 2, (g + 1) * GT % (RG * GT), g == 0)
                hidden(g, g % 2, g < 2)

            pe.wait_ge(par2_in, 32)

            def graph_out(g, b):
                pe.wait_ge(out_ev, g - 1)
                for h in range(HALVES):
                    pe.wait_ge(relu_ok, g * 2 + (h + 1))
                    ins = mm(psA[b], gw2s[:, h, :], hid[h][:, ds(g * GC, GC)], start=(h == 0), stop=(h == HALVES - 1))
                ins.then_inc(out_mm, 1)

            for g in range(2):
                pe.wait_ge(relu_ok, 2 * g + 2)
                for h in range(HALVES):
                    ins = mm(psA[g], gw2s[:, h, :], hid[h][:, g * GC:(g + 1) * GC], start=(h == 0), stop=(h == HALVES - 1))
                ins.then_inc(out_mm, 1)
            with pe.Fori(1, GR // 2) as j:
                graph_out(j * 2, 0)
                graph_out(j * 2 + 1, 1)

            def back_to_rows(*groups):
                for g in range(*groups):
                    pe.wait_ge(bnout, g + 1)
                    if g >= 3:
                        pe.wait_ge(x2_ok, g - 2)
                    for u in range(GT):
                        ins = nc.tensor.transpose(psT[g % 3][:, u * P:(u + 1) * P],
                                                  gout[:, g * GC + u * P:g * GC + (u + 1) * P], ident[:, :])
                    ins.then_inc(outT_mm, 1)

            def z_cols(g, b, first=False):
                pe.wait_ge(z_ok, g + 1)
                pe.wait_ge(z_dve, g + 1)
                if not first:
                    pe.wait_ge(zr_ev, g - 1)
                for u in range(GT):
                    ins = nc.tensor.transpose(psZ[b][:, u * P:(u + 1) * P], zrow[:, g * GT + u, 0:C], ident[:, :])
                ins.then_inc(zr_mm, 1)

            def logits(g, b, c):
                pe.wait_ge(zr_ev, g + 1)
                for u in range(GT):
                    ins = mm(psL[c % 2][:, ds((g * GT + (u - chunk0[c])) * E, E)], zTr[:, b, u * P:(u + 1) * P],
                             rws[:, :], start=True, stop=True)
                ins.then_inc(logit_mm, 1)

            def ranks(c):
                n = E * CHUNKS[c]
                pe.wait_ge(sel_ok, c + 1)
                if c:
                    pe.wait_ge(routed, c)
                mm(psR[:, 0:n], before[:, :], tmp[3][:, 0:n], start=True, stop=True)
                mm(psR[:, n:2 * n], ones[:, :], tmp[3][:, 0:n], start=True, stop=True).then_inc(rank_mm, 1)

            def columns(p, c, rows=None, ranks_of=None):
                g0, g1 = PARTS[p]
                if c >= 2:
                    pe.wait_ge(routed, c - 1)
                for g in range(g0, g1):
                    z_cols(g, g % 2, g < 2)
                    if g > g0:
                        logits(g - 1, (g - 1) % 2, c)
                    if rows is not None and g == g0:
                        back_to_rows(*rows)
                    if ranks_of is not None and g == g0 + 1:
                        ranks(ranks_of)
                logits(g1 - 1, (g1 - 1) % 2, c)

            back_to_rows(0, G[1] + 3)
            columns(0, 0, rows=(G[1] + 3, MID))
            back_to_rows(MID, MID + 3)
            columns(1, 1, ranks_of=0)
            back_to_rows(MID + 3, G[2] + 2)
            columns(2, 1, rows=(G[2] + 2, GR))
            columns(3, 2, ranks_of=1)
            ranks(2)
            pe.wait_ge(etab_ok, len(CHUNKS))
            pe.wait_ge(split, 4 * E + 1)

            def zT(g, i, turn, first=False):
                if not first:
                    pe.wait_ge(zl_ok, g)
                if i % UNIT == 0:
                    pe.wait_ge(slot_in[i // UNIT], turn)
                nc.tensor.transpose(psz, zslot[:, i, 0:C], ident[:, :]).then_inc(zT_mm, 1)

            def w13_at(e, part, c0, n):
                return w13s[:, ds(e * (4 * HF) + (part * 2 * HF + c0), n)]

            def w2_at(e, j, k):
                return w2s[0:k, ds(e * (6 * C) + j * 2 * C, 2 * C)]

            def h13(g, i, e):
                b = i % 2
                cols = ((ps13[b][:, 0:HA], 0, HA), (ps13[b][:, HA:2 * HF], HA, HB))
                for z, part, st, sp_ in ((zTh, 0, True, False), (zTh, 1, False, False), (zTl, 0, False, True)):
                    for o, c0, n in cols:
                        ins = mm(o, z[:, b, :], w13_at(e, part, c0, n), start=st, stop=sp_)
                ins.then_inc(h13_mm, 1)

            def hT(g, i, first=False):
                pe.wait_ge(h_ok, g + 1)
                if not first:
                    pe.wait_ge(hTl_ok, g)
                for j in range(3):
                    ins = nc.tensor.transpose(psh[:, j * P:(j + 1) * P], hsl[:, i % 2, j * KC:(j + 1) * KC], ident[:, :])
                ins.then_inc(hT_mm, 1)

            def y(g, i, e, first=False):
                if not first:
                    pe.wait_ge(y_ev, g - 1)
                for j, k in enumerate(KJ):
                    for h in (hTh, hTl):
                        ins = mm(psy[i % 2], h[0:k, i % 2, j * P:(j + 1) * P], w2_at(e, j, k),
                                 start=(j == 0 and h is hTh), stop=(j == 2 and h is hTl))
                ins.then_inc(y_mm, 1)

            def experts(g, n):
                return nc.values_load_multi_w_load_instructions(
                    etab[0:1, ds(g, n)], engines=(mybir.EngineType.PE,), min_val=0, max_val=E - 1,
                    skip_runtime_bounds_check_because="the table is clamped to E - 1 and counts from 0")[1]

            def addresses(e, e2):
                if e is not None:
                    for part in range(2):
                        for c0, n in ((0, HA), (HA, HB)):
                            pe.lower_ap(w13_at(e, part, c0, n))
                if e2 is not None:
                    for j, k in enumerate(KJ):
                        pe.lower_ap(w2_at(e2, j, k))

            zT(0, 0, 16, True)
            ex = experts(0, RING)
            for g in range(RING):
                zT(g + 1, (g + 1) % RING, 16 * ((g + 1) // RING + 1))
                h13(g, g, ex[g])
                if g >= 1:
                    hT(g - 1, g - 1, g == 1)
                if g >= 2:
                    y(g - 2, g - 2, ex[g - 2], g - 2 < 2)
            held = [pe.alloc_register(f"expert{i}") for i in range(RING)]
            HR = RING // 2
            pe.load(held[HR:], etab[0:1, HR:RING])
            pe.load(held[:HR], etab[0:1, RING:RING + HR])
            with pe.Fori(1, NS // RING - 1) as r:
                slot_of = lambda i: pe.snap(held[i], min_val=0, max_val=E - 1)
                ex = [slot_of(RING - 2), slot_of(RING - 1)]
                for i in range(RING):
                    g = r * RING + i
                    ex.append(slot_of(i))
                    addresses(ex[i + 2], ex[i])
                    zT(g + 1, (i + 1) % RING, r * 16 + (16 if i < RING - 1 else 32))
                    h13(g, i, ex[i + 2])
                    if i == 2:
                        pe.load(held[HR:], etab[0:1, ds(r * RING + HR, HR)])
                    if i == RING - 2:
                        pe.load(held[:HR], etab[0:1, ds(r * RING + RING, HR)])
                    hT(g - 1, i - 1)
                    y(g - 2, i - 2, ex[i])
            ex = experts(NS - RING - 4, RING + 4)
            for i in range(RING + 2):
                g = NS - RING + i
                if i < RING - 1:
                    zT(g + 1, i + 1, 16 * (NS // RING))
                if i == RING - 1:
                    pe.wait_ge(zl_ok, NS)
                if i < RING:
                    h13(g, i, ex[i + 4])
                if i < RING + 1:
                    hT(g - 1, i - 1)
                else:
                    pe.wait_ge(hTl_ok, NS)
                y(g - 2, i - 2, ex[i + 2])


def kernel(x, adj, L0_gnn_W1, L0_gnn_b1, L0_gnn_g1, L0_gnn_be1, L0_gnn_W2, L0_gnn_b2, L0_gnn_g2, L0_gnn_be2,
           L0_ffn_router_w, L0_ffn_w1, L0_ffn_w2, L0_ffn_w3):
    import numpy as np
    import concourse.bacc as bacc
    from concourse import mybir
    from concourse.bass_utils import run_bass_kernel_spmd as run

    c = np.ascontiguousarray
    a = lambda v: np.asarray(v)
    cols = lambda v: a(v).reshape(-1, P).T
    w13 = np.concatenate([a(L0_ffn_w1), a(L0_ffn_w3)], axis=1)
    arrays = {
        "x_rows": c(a(x).reshape(TOK, C)),
        "adj_in": c(a(adj)),
        "gnn_w1_t": c(a(L0_gnn_W1).T),
        "gnn_w2_t": c(a(L0_gnn_W2).T),
        "gnn_vectors": c(np.concatenate([cols(L0_gnn_b1), cols(L0_gnn_g1), cols(L0_gnn_be1), cols(L0_gnn_b2),
                                         cols(L0_gnn_g2), cols(L0_gnn_be2)], axis=1)),
        "router_t": c(a(L0_ffn_router_w).T),
        "w13_t": c(w13.transpose(2, 0, 1).reshape(C, E * 2 * HF)),
        "w2_t": c(a(L0_ffn_w2).transpose(0, 2, 1).reshape(E * HF, C)),
    }
    nc = bacc.Bacc("TRN2", target_bir_lowering=False, num_devices=1)
    args = [nc.dram_tensor(k, v.shape, mybir.dt.from_np(v.dtype), kind="ExternalInput").ap() for k, v in arrays.items()]
    out = nc.dram_tensor("out_rows", (TOK, C), mybir.dt.float32, kind="ExternalOutput").ap()
    build(nc, *args, out)
    got = run(nc, [arrays], core_ids=[0])
    return got.results[0]["out_rows"].reshape(B, N, C)
```
